# Optimizing a Trainium2 kernel written in Bass

```python
import numpy as np
import jax
import jax.numpy as jnp

def _softmax(x, axis=-1):
    return jax.nn.softmax(x, axis=axis)
def _gelu(x):
    return jax.nn.gelu(x, approximate=True)
def _silu(x):
    return jax.nn.silu(x)
def _sigmoid(x):
    return jax.nn.sigmoid(x)
def _layernorm(x, axis=-1, eps=1e-5):
    m = jnp.mean(x, axis=axis, keepdims=True)
    v = jnp.var(x, axis=axis, keepdims=True)
    return (x - m) / jnp.sqrt(v + eps)
def _scatter_add(tgt, idx, src, axis=0):
    return tgt.at[idx].add(src)
def _segment_sum(src, seg, n):
    return jax.ops.segment_sum(src, seg, n)

kernel_name = 'mk_conv_seq_d2_conv_nchw128_6e939a'

def setup_inputs(seed: int = 0):
    np.random.seed(seed)
    _w = jnp.asarray
    def _rec_inputs():
        import jax
        import jax.numpy as jnp
        _gk = jax.random.key(seed)
        x = -0.0005207 + 1.001 * jax.random.normal(jax.random.fold_in(_gk, 1), (4, 128, 64, 64), jnp.float32)
        return x
    x = _rec_inputs()
    def _L0_conv_setup():
        import jax, jax.numpy as jnp
        import numpy as np
        B, C, H, W = (4, 128, 64, 64)
        HEADS = 4
        HD = C // HEADS
        HIDDEN = 2 * C
        EPS = 1e-05

        def layernorm(x, w, b):
            mu = jnp.mean(x, axis=-1, keepdims=True)
            var = jnp.mean(jnp.square(x - mu), axis=-1, keepdims=True)
            return (x - mu) * jax.lax.rsqrt(var + EPS) * w + b
        key = jax.random.key(seed)
        ks = jax.random.split(key, 8)
        s = 0.02
        return {'x': jax.random.normal(ks[0], (B, C, H, W), dtype=jnp.float32), 'ln1_w': jnp.ones((C,), jnp.float32), 'ln1_b': jnp.zeros((C,), jnp.float32), 'qkv_w': jax.random.normal(ks[1], (3 * C, C), jnp.float32) * s, 'proj_w': jax.random.normal(ks[2], (C, C), jnp.float32) * s, 'proj_b': jnp.zeros((C,), jnp.float32), 'ln2_w': jnp.ones((C,), jnp.float32), 'ln2_b': jnp.zeros((C,), jnp.float32), 'fc1_w': jax.random.normal(ks[3], (HIDDEN, C), jnp.float32) * s, 'fc1_b': jnp.zeros((HIDDEN,), jnp.float32), 'fc2_w': jax.random.normal(ks[4], (C, HIDDEN), jnp.float32) * s, 'fc2_b': jnp.zeros((C,), jnp.float32)}
    _L0_conv_all = _L0_conv_setup()
    _L0_conv_in = {k: v for k, v in _L0_conv_all.items() if k in ('ln1_w', 'ln1_b', 'qkv_w', 'proj_w', 'proj_b', 'ln2_w', 'ln2_b', 'fc1_w', 'fc1_b', 'fc2_w', 'fc2_b', )}
    del _L0_conv_all

    def _L1_conv_setup():
        import jax, jax.numpy as jnp
        import numpy as np
        TOKEN_NUM = 8
        GCN = 16
        D_INNER = 32
        D_STATE = 16
        D_CONV = 4
        DT_RANK = 1
        GROUPS = 4
        EPS = 1e-05

        def _mamba(seq, in_proj_w, conv1d_w, conv1d_b, x_proj_w, dt_proj_w, dt_proj_b, A_log, D, out_proj_w):
            xz = jnp.einsum('nld,ed->nle', seq, in_proj_w)
            xi, z = jnp.split(xz, 2, axis=-1)
            xc = jax.lax.conv_general_dilated(xi.transpose(0, 2, 1), conv1d_w, (1,), ((D_CONV - 1, 0),), dimension_numbers=('NCH', 'OIH', 'NCH'), feature_group_count=D_INNER)
            xc = jax.nn.silu((xc + conv1d_b[None, :, None]).transpose(0, 2, 1))
            xdbl = jnp.einsum('nld,ed->nle', xc, x_proj_w)
            dt, Bm, Cm = jnp.split(xdbl, [DT_RANK, DT_RANK + D_STATE], axis=-1)
            dt = jax.nn.softplus(jnp.einsum('nlr,dr->nld', dt, dt_proj_w) + dt_proj_b)
            A = -jnp.exp(A_log)
            dA = jnp.exp(dt[..., None] * A)
            dBx = dt[..., None] * Bm[:, :, None, :] * xc[..., None]

            def step(h, inp):
                a, b, c = inp
                h = a * h + b
                return (h, jnp.sum(h * c[:, None, :], axis=-1))
            h0 = jnp.zeros((seq.shape[0], D_INNER, D_STATE), dA.dtype)
            _, ys = jax.lax.scan(step, h0, (dA.transpose(1, 0, 2, 3), dBx.transpose(1, 0, 2, 3), Cm.transpose(1, 0, 2)))
            ym = ys.transpose(1, 0, 2) + D * xc
            ym = ym * jax.nn.silu(z)
            return jnp.einsum('nld,ed->nle', ym, out_proj_w)
        key = jax.random.key(seed)
        ks = jax.random.split(key, 8)
        g = lambda k, shape, scale: jax.random.normal(k, shape, jnp.float32) * scale
        d = {}
        d['x'] = jax.random.normal(ks[0], (2, 128, 128, 128), jnp.float32)
        d['conv_w'] = g(ks[1], (128, 128, 3, 3), 0.03)
        d['conv_b'] = jnp.zeros((128,), jnp.float32)
        d['gn_w'] = jnp.ones((128,), jnp.float32)
        d['gn_b'] = jnp.zeros((128,), jnp.float32)
        d['in_proj_w'] = g(ks[2], (2 * D_INNER, GCN), 0.25)
        d['conv1d_w'] = g(ks[3], (D_INNER, 1, D_CONV), 0.3)
        d['conv1d_b'] = jnp.zeros((D_INNER,), jnp.float32)
        d['x_proj_w'] = g(ks[4], (DT_RANK + 2 * D_STATE, D_INNER), 0.18)
        d['dt_proj_w'] = g(ks[5], (D_INNER, DT_RANK), 1.0)
        d['dt_proj_b'] = jnp.full((D_INNER,), -2.0, jnp.float32)
        d['A_log'] = jnp.tile(jnp.log(jnp.arange(1, D_STATE + 1, dtype=jnp.float32)), (D_INNER, 1))
        d['D'] = jnp.ones((D_INNER,), jnp.float32)
        d['out_proj_w'] = g(ks[6], (GCN, D_INNER), 0.18)
        return d
    _L1_conv_all = _L1_conv_setup()
    _L1_conv_in = {k: v for k, v in _L1_conv_all.items() if k in ('conv_w', 'conv_b', 'gn_w', 'gn_b', 'in_proj_w', 'conv1d_w', 'conv1d_b', 'x_proj_w', 'dt_proj_w', 'dt_proj_b', 'A_log', 'D', 'out_proj_w', )}
    del _L1_conv_all

    return {
        "x": x,
        "L0_conv_ln1_w": _L0_conv_in["ln1_w"],
        "L0_conv_ln1_b": _L0_conv_in["ln1_b"],
        "L0_conv_qkv_w": _L0_conv_in["qkv_w"],
        "L0_conv_proj_w": _L0_conv_in["proj_w"],
        "L0_conv_proj_b": _L0_conv_in["proj_b"],
        "L0_conv_ln2_w": _L0_conv_in["ln2_w"],
        "L0_conv_ln2_b": _L0_conv_in["ln2_b"],
        "L0_conv_fc1_w": _L0_conv_in["fc1_w"],
        "L0_conv_fc1_b": _L0_conv_in["fc1_b"],
        "L0_conv_fc2_w": _L0_conv_in["fc2_w"],
        "L0_conv_fc2_b": _L0_conv_in["fc2_b"],
        "L1_conv_conv_w": _L1_conv_in["conv_w"],
        "L1_conv_conv_b": _L1_conv_in["conv_b"],
        "L1_conv_gn_w": _L1_conv_in["gn_w"],
        "L1_conv_gn_b": _L1_conv_in["gn_b"],
        "L1_conv_in_proj_w": _L1_conv_in["in_proj_w"],
        "L1_conv_conv1d_w": _L1_conv_in["conv1d_w"],
        "L1_conv_conv1d_b": _L1_conv_in["conv1d_b"],
        "L1_conv_x_proj_w": _L1_conv_in["x_proj_w"],
        "L1_conv_dt_proj_w": _L1_conv_in["dt_proj_w"],
        "L1_conv_dt_proj_b": _L1_conv_in["dt_proj_b"],
        "L1_conv_A_log": _L1_conv_in["A_log"],
        "L1_conv_D": _L1_conv_in["D"],
        "L1_conv_out_proj_w": _L1_conv_in["out_proj_w"],
    }

def reference(x, L0_conv_ln1_w, L0_conv_ln1_b, L0_conv_qkv_w, L0_conv_proj_w, L0_conv_proj_b, L0_conv_ln2_w, L0_conv_ln2_b, L0_conv_fc1_w, L0_conv_fc1_b, L0_conv_fc2_w, L0_conv_fc2_b, L1_conv_conv_w, L1_conv_conv_b, L1_conv_gn_w, L1_conv_gn_b, L1_conv_in_proj_w, L1_conv_conv1d_w, L1_conv_conv1d_b, L1_conv_x_proj_w, L1_conv_dt_proj_w, L1_conv_dt_proj_b, L1_conv_A_log, L1_conv_D, L1_conv_out_proj_w):
    import jax
    import jax.numpy as jnp
    def _L0_conv_ref(x, ln1_w, ln1_b, qkv_w, proj_w, proj_b, ln2_w, ln2_b, fc1_w, fc1_b, fc2_w, fc2_b):
        import jax, jax.numpy as jnp
        import numpy as np
        B, C, H, W = (4, 128, 64, 64)
        HEADS = 4
        HD = C // HEADS
        HIDDEN = 2 * C
        EPS = 1e-05

        def layernorm(x, w, b):
            mu = jnp.mean(x, axis=-1, keepdims=True)
            var = jnp.mean(jnp.square(x - mu), axis=-1, keepdims=True)
            return (x - mu) * jax.lax.rsqrt(var + EPS) * w + b
        b, c, h, w = x.shape
        n = h * w
        x_ln = layernorm(jnp.transpose(x, (0, 2, 3, 1)), ln1_w, ln1_b)
        qkv = jnp.einsum('bhwc,oc->bohw', x_ln, qkv_w)
        q, k, v = jnp.split(qkv, 3, axis=1)
        q = q.reshape(b, HEADS, HD, n)
        k = k.reshape(b, HEADS, HD, n)
        v = v.reshape(b, HEADS, HD, n)
        scale = 1.0 / jnp.sqrt(jnp.float32(HD))
        scores = jnp.einsum('bhdn,bhdm->bhnm', q, k) * scale
        attn = jax.nn.softmax(scores, axis=-1)
        out = jnp.einsum('bhnm,bhdm->bhdn', attn, v)
        out = out.reshape(b, c, h, w)
        out = jnp.einsum('bchw,oc->bohw', out, proj_w) + proj_b[None, :, None, None]
        x = x + out
        x_ln2 = layernorm(jnp.transpose(x, (0, 2, 3, 1)), ln2_w, ln2_b)
        x_flat = x_ln2.reshape(b, n, c)
        hdn = jax.nn.gelu(jnp.einsum('bnc,oc->bno', x_flat, fc1_w) + fc1_b, approximate=False)
        x_mlp = jnp.einsum('bno,co->bnc', hdn, fc2_w) + fc2_b
        x_mlp = jnp.transpose(x_mlp.reshape(b, h, w, c), (0, 3, 1, 2))
        return x + x_mlp

    def _L1_conv_ref(x, conv_w, conv_b, gn_w, gn_b, in_proj_w, conv1d_w, conv1d_b, x_proj_w, dt_proj_w, dt_proj_b, A_log, D, out_proj_w):
        import jax, jax.numpy as jnp
        import numpy as np
        TOKEN_NUM = 8
        GCN = 16
        D_INNER = 32
        D_STATE = 16
        D_CONV = 4
        DT_RANK = 1
        GROUPS = 4
        EPS = 1e-05

        def _mamba(seq, in_proj_w, conv1d_w, conv1d_b, x_proj_w, dt_proj_w, dt_proj_b, A_log, D, out_proj_w):
            xz = jnp.einsum('nld,ed->nle', seq, in_proj_w)
            xi, z = jnp.split(xz, 2, axis=-1)
            xc = jax.lax.conv_general_dilated(xi.transpose(0, 2, 1), conv1d_w, (1,), ((D_CONV - 1, 0),), dimension_numbers=('NCH', 'OIH', 'NCH'), feature_group_count=D_INNER)
            xc = jax.nn.silu((xc + conv1d_b[None, :, None]).transpose(0, 2, 1))
            xdbl = jnp.einsum('nld,ed->nle', xc, x_proj_w)
            dt, Bm, Cm = jnp.split(xdbl, [DT_RANK, DT_RANK + D_STATE], axis=-1)
            dt = jax.nn.softplus(jnp.einsum('nlr,dr->nld', dt, dt_proj_w) + dt_proj_b)
            A = -jnp.exp(A_log)
            dA = jnp.exp(dt[..., None] * A)
            dBx = dt[..., None] * Bm[:, :, None, :] * xc[..., None]

            def step(h, inp):
                a, b, c = inp
                h = a * h + b
                return (h, jnp.sum(h * c[:, None, :], axis=-1))
            h0 = jnp.zeros((seq.shape[0], D_INNER, D_STATE), dA.dtype)
            _, ys = jax.lax.scan(step, h0, (dA.transpose(1, 0, 2, 3), dBx.transpose(1, 0, 2, 3), Cm.transpose(1, 0, 2)))
            ym = ys.transpose(1, 0, 2) + D * xc
            ym = ym * jax.nn.silu(z)
            return jnp.einsum('nld,ed->nle', ym, out_proj_w)
        B, C, H, W = x.shape
        y = jax.lax.conv_general_dilated(x, conv_w, (1, 1), ((1, 1), (1, 1)), dimension_numbers=('NCHW', 'OIHW', 'NCHW'))
        y = y + conv_b[None, :, None, None]
        seq = y.reshape(B * H * W, TOKEN_NUM, GCN)
        out = _mamba(seq, in_proj_w, conv1d_w, conv1d_b, x_proj_w, dt_proj_w, dt_proj_b, A_log, D, out_proj_w)
        xr = out.reshape(B, C, H, W)
        g = xr.reshape(B, GROUPS, C // GROUPS, H, W)
        mu = g.mean((2, 3, 4), keepdims=True)
        var = g.var((2, 3, 4), keepdims=True)
        g = (g - mu) / jnp.sqrt(var + EPS)
        xp = g.reshape(B, C, H, W) * gn_w[None, :, None, None] + gn_b[None, :, None, None]
        xp = jax.nn.silu(xp)
        return x + xp

    def _gn(v, G=32, eps=1e-5):
        B_, C_, H_, W_ = v.shape
        g = v.reshape(B_, G, C_ // G, H_, W_)
        m = jnp.mean(g, axis=(2, 3, 4), keepdims=True)
        s = jnp.var(g, axis=(2, 3, 4), keepdims=True)
        return ((g - m) / jnp.sqrt(s + eps)).reshape(v.shape)

    def _ln_c(v, eps=1e-6):
        m = jnp.mean(v, axis=1, keepdims=True)
        s = jnp.var(v, axis=1, keepdims=True)
        return (v - m) / jnp.sqrt(s + eps)

    def _ln_t(v, eps=1e-5):
        m = jnp.mean(v, axis=-1, keepdims=True)
        s = jnp.var(v, axis=-1, keepdims=True)
        return (v - m) / jnp.sqrt(s + eps)

    def _to_tokens(v):
        B_, C_, H_, W_ = v.shape
        return v.reshape(B_, C_, H_ * W_).transpose(0, 2, 1)
    def _from_tokens(t, like):
        B_, C_, H_, W_ = like.shape
        return t.transpose(0, 2, 1).reshape(B_, C_, H_, W_)

    x = _L0_conv_ref(x, L0_conv_ln1_w, L0_conv_ln1_b, L0_conv_qkv_w, L0_conv_proj_w, L0_conv_proj_b, L0_conv_ln2_w, L0_conv_ln2_b, L0_conv_fc1_w, L0_conv_fc1_b, L0_conv_fc2_w, L0_conv_fc2_b)
    x = _L1_conv_ref(x, L1_conv_conv_w, L1_conv_conv_b, L1_conv_gn_w, L1_conv_gn_b, L1_conv_in_proj_w, L1_conv_conv1d_w, L1_conv_conv1d_b, L1_conv_x_proj_w, L1_conv_dt_proj_w, L1_conv_dt_proj_b, L1_conv_A_log, L1_conv_D, L1_conv_out_proj_w)
    return x


_drawn_inputs = setup_inputs


def setup_inputs(seed=0):
    import zlib

    import numpy as np

    out = dict(_drawn_inputs(seed))
    spreads = {'L0_conv_ln1_w': (1.0, 0.6),
     'L0_conv_ln1_b': (0.0, 0.8),
     'L0_conv_proj_b': (0.0, 0.393),
     'L0_conv_ln2_w': (1.0, 0.6),
     'L0_conv_ln2_b': (0.0, 2.0),
     'L0_conv_fc1_b': (0.0, 2.0),
     'L0_conv_fc2_b': (0.0, 0.443),
     'L1_conv_conv_b': (0.0, 0.8),
     'L1_conv_gn_w': (1.0, 0.6),
     'L1_conv_gn_b': (0.0, 0.8),
     'L1_conv_conv1d_b': (0.0, 0.8),
     'L1_conv_dt_proj_b': (-2.0, 0.6),
     'L1_conv_D': (1.0, 0.6)}
    factors = {'L0_conv_qkv_w': 8.0, 'L0_conv_proj_w': 8.0, 'L1_conv_A_log': 3.27, 'L0_conv_fc1_w': 4.399}
    for name, (base, spread) in spreads.items():
        noise = np.random.default_rng([zlib.crc32(name.encode()), seed]).standard_normal(out[name].shape)
        drawn = base * np.exp(spread * noise) if base else spread * noise
        out[name] = jnp.asarray(drawn.astype(out[name].dtype))
    for name, factor in factors.items():
        out[name] = (out[name] * factor).astype(out[name].dtype)
    return out
```

```python
from contextlib import ExitStack

import numpy as np

import concourse.bass as bass
from concourse import mybir

F32 = mybir.dt.float32
F16 = mybir.dt.float16
BF16 = mybir.dt.bfloat16
ALU = mybir.AluOpType
ACT = mybir.ActivationFunctionType
AX = mybir.AxisListType

C = 128
HEADS, HD = 4, 32
SIDE = 64
PAD = SIDE + 2
N = SIDE * SIDE
TC = 512
NCH = N // TC
ROWS = TC // SIDE
NJ = HEADS * NCH
KB = N // 128
UNITS = KB // 2
LAG = 3
NB = 4
TILES = 4 * NCH
EPS = 1e-5
QS = 16.0
SCALE = 1.0 / (QS * QS * float(np.sqrt(HD)))
ROW = 256.0
SHIFT = 14 * float(np.log(2)) / (SCALE * ROW)
CAST = "AAAADAAAADAAAAAD"
SUB = "PDPPDPPDPPDPPDPD"


def upto(table, key, u):
    return sum(t == key for t in table[:u + 1])


CAST_D = CAST.count("D")
SUB_P, SUB_D = SUB.count("P"), SUB.count("D")

START = 1

L, F, E, ST_N, DCONV = 8, 16, 32, 16, 4
NQ = SIDE // 4
SEQ = 2 * C
COLS = L * SEQ
GR = E * ST_N // 128
PARTS = 3
GROUPS = 4
HC_DVE = {3}
CHAIN = 14

VECS = ["ln1_w", "ln1_b", "ln2_w", "ln2_b", "fc1_b0", "fc1_b1", "fc2_b", "eps",
        "conv_b", "gn_w", "gn_b", "conv1d_b", "dt_b", "D"]
WIDTHS = {"mean": 128, "ident": 128, "wq": 384, "wk": 384, "wv": 128, "proj": 512, "spread": 128, "head_bias": 4,
          "w1": 256, "w2": 256, "vecs": len(VECS), "conv": 9 * 128, "xi": 256, "z": 256, "dt": 128, "bc": 128,
          "out": 64, "sum": 128, "group": 128, "A": GR}
RAW = {"conv1d": 256, "dt_row": 128, "spread_e": 512, "spread_b": 128, "spread_c": 128}


def build(nc, x_in, consts_in, raw_in, out, B):
    at, pos, raw_at, raw_pos = {}, 0, {}, 0
    for k, width in WIDTHS.items():
        at[k] = pos
        pos += width
    for k, width in RAW.items():
        raw_at[k] = raw_pos
        raw_pos += width
    with ExitStack() as ctx:
        sb = lambda name, shape, dt=F32: ctx.enter_context(nc.sbuf_tensor(name, shape, dt))
        sem = lambda name: ctx.enter_context(nc.semaphore(name))

        cst = sb("cst", [128, pos])
        x = sb("x", [128, N])
        x2 = sb("x2", [128, PAD, PAD])
        spread = sb("spread_bf", [128, 768], BF16)
        negA = sb("negA", [128, GR])
        ARENA = 148 * 256
        arena = sb("arena", [128, ARENA])
        used = [0]

        def take(shape, dt=F32):
            size = int(np.prod(shape)) // (1 if dt == F32 else 2)
            assert used[0] + size <= ARENA, (used[0] + size, ARENA)
            a = arena[:, used[0]:used[0] + size]
            used[0] += size
            if dt != F32:
                a = a.bitcast(dt)
            if len(shape) == 2:
                a = a.rearrange("p (a b) -> p a b", a=shape[0])
            elif len(shape) == 3:
                a = a.rearrange("p (a b c) -> p a b c", a=shape[0], b=shape[1])
            return a

        qst = take([HEADS * N], F16)
        kst = take([HEADS * N], F16)
        vst = take([HEADS * KB * 128], BF16)
        at_p = used[0]
        p32 = take([NB, 1024])
        p1 = take([NB, 1024], F16)
        p2 = take([NB, 1024], F16)
        osb, lns, rcp = take([TC]), take([TC]), take([TC])
        onrm = take([TC])[0:96, :]
        mx, cneg = take([TILES]), take([4])
        crow = take([128])[0:4, :]
        chi, clo = take([128], F16)[0:4, :], take([128], F16)[0:4, :]
        pcur = take([128])[0:96, :]
        used[0] = at_p
        xc, sq, rstd, z, xln, hid = (take([2, TC]) for _ in range(6))
        lnv, vres = take([TC]), take([TC])
        used[0] = 0
        dA, dbx = take([2, COLS]), take([2, COLS])
        hs = take([COLS])
        hC = take([2, COLS])
        bsb, csb = take([COLS]), take([COLS])
        stk = {k: take([2, COLS], BF16) for k in ("dt", "u", "bc")}
        pcs = {k: take([PARTS, TC], BF16) for k in ("dt", "u", "bc")}
        yc, yT = take([SEQ]), take([SEQ])
        xcs, szs = take([4, TC]), take([4, TC])
        mdt, edt, ldt, dts, us, rbc, rdt, ru, ya, ym = (take([TC]) for _ in range(10))
        gs = take([16])
        used[0] = 0
        raw = take([raw_pos])
        used[0] = 0
        xp, junk, fin = take([N]), take([N]), take([N])
        xr = x
        ps = ctx.enter_context(nc.psum_tensor("ps", [128, 8, TC], F32))

        w = lambda k: cst[:, at[k]:at[k] + WIDTHS[k]]
        vec = lambda k: cst[:, at["vecs"] + VECS.index(k):at["vecs"] + VECS.index(k) + 1]

        S = {n: sem("s_" + n) for n in (
            "cst x init mean xc sq var ln rstd z xln xlnfree qk q1 q2 v v1 vr v2 v3 "
            "sm red cneg ct crow chi clo cdma st p32 p1d subp subd pv oev lns rcp bc on pcur proj tbfree "
            "fc1 gelu fc2 x2 out seen fill "
            "raw prep dz conv yc tr yT xi zz xcs szs dtp bcp bc1 rbc m e l dt chain pcs sdt su sbc "
            "bcu bcev dtu uu da dbx scan hcp hcd y ya ym outp xr gsum gmm gmu gsq gvv gln grs gsc gxp fin gsc2 step").split()}
        (s_cst, s_x, s_init, s_mean, s_xc, s_sq, s_var, s_ln, s_rstd, s_z, s_xln, s_xlnfree, s_qk, s_q1, s_q2, s_v, s_v1,
         s_vr, s_v2, s_v3, s_sm, s_red, s_cneg, s_ct, s_crow, s_chi, s_clo, s_cdma, s_st, s_p32, s_p1d,
         s_subp, s_subd, s_pv, s_oev, s_lns, s_rcp, s_bc, s_on, s_pcur, s_proj, s_tbfree, s_fc1, s_gelu,
         s_fc2, s_x2, s_out, s_seen, s_fill, s_raw, s_prep, s_dz, s_conv, s_yc, s_tr, s_yT, s_xi, s_zz, s_xcs, s_szs,
         s_dtp, s_bcp, s_bc1, s_rbc, s_m, s_e, s_l, s_dt, s_chain, s_pcs, s_sdt, s_su, s_sbc, s_bcu, s_bcev, s_dtu,
         s_uu, s_da, s_dbx, s_scan, s_hcp, s_hcd, s_y, s_ya, s_ym, s_outp, s_xr, s_gsum, s_gmm, s_gmu, s_gsq,
         s_gvv, s_gln, s_grs, s_gsc, s_gxp, s_fin, s_gsc2, s_step) = S.values()

        MEAN, VAR, QK, VB = 0, 1, 2, 6
        ST, SM, OB, TB = 0, 4, 6, 7
        FC1, FC2 = 2, 4
        DT, UU, YB, SA, SB = 0, 2, 4, 6, 7

        block = ctx.enter_context(nc.Block())
        ds = bass.ds

        def slot(t, f):
            return t.rearrange("p a b -> p (a b)")[:, ds((f & 3) * TC, TC)]

        def stack(k, q, n):
            return stk[k].rearrange("p a b -> p (a b)")[0:96, ds((q & 1) * COLS + n * TC, TC)]

        def times_c(eng, api, Q, g, first, done):
            
            eng.wait_ge(s_scan, Q * GR + g + 1)
            if g == min(set(range(GR)) - HC_DVE) or g in HC_DVE:
                eng.wait_ge(s_bcev, Q * 8 + 8)
            if not (first and g < 2):
                eng.wait_ge(s_y, Q * GR + g - 1)
            api.tensor_tensor(hC[:, g % 2, :].rearrange("p (t n) -> p t n", t=L),
                              hs[:, :].rearrange("p (n t) -> p t n", t=L),
                              csb[:, :].rearrange("p (t n) -> p t n", t=L), ALU.mult).then_inc(done, 1)

        def v_psum():
            return ps[:, VB, :].rearrange("p (k h d) -> p k h d", k=4, h=HEADS)

        def v_part(part, i):
            v = vst[:, :].rearrange("p (h k m) -> p k h m", h=HEADS, k=KB)
            return v[:, ds(i * 4, 4), :, HD * part:HD * part + HD]

        def vres4():
            return vres[:, :].rearrange("p (k h d) -> p k h d", k=4, h=HEADS)

        def head_base(j):
            return (j & (NJ - NCH)) * TC

        def chunks(eng, body):
            with eng.Fori(0, NCH // 2 - 1) as t:
                body(2 * t, 0, True)
                body(2 * t + 1, 1, True)
            body(NCH - 2, 0, True)
            body(NCH - 1, 1, False)

        def mchunks(eng, body):
            body(0, True, True)
            with eng.Fori(0, NQ - 3) as t:
                body(t + 1, False, True)
            body(NQ - 2, False, False)
            body(NQ - 1, False, False)

        HCD, HCP = len(HC_DVE), GR - len(HC_DVE)

        def wait_hc(eng, Q, g):
            if g in HC_DVE:
                eng.wait_ge(s_hcd, Q * HCD + sum(i in HC_DVE for i in range(g + 1)))
            else:
                eng.wait_ge(s_hcp, Q * HCP + sum(i not in HC_DVE for i in range(g + 1)))

        def tn(t, k):
            return t.rearrange("p (n t) -> p t n", t=L)[:, 2 * k:2 * k + 2, :]

        def qchunks(eng, body):
            body(0, True, True, True)
            with eng.Fori(0, NJ - 3) as t:
                body(t + 1, False, True, True)
            body(NJ - 2, False, True, False)
            body(NJ - 1, False, False, False)

        @block.tensor
        def _(pe):
            def mean(i, L):
                pe.wait_ge(s_xc, START + L)
                nc.tensor.matmul(ps[:, MEAN, :], w("mean"), x[:, ds(i * TC, TC)],
                                 start=True, stop=True).then_inc(s_mean, 1)

            def var(par, L):
                pe.wait_ge(s_sq, L + 1)
                pe.wait_ge(s_ln, START + L)
                nc.tensor.matmul(ps[:, VAR, :], w("mean"), sq[:, par, :],
                                 start=True, stop=True).then_inc(s_var, 1)

            def project(par, K, which):
                for h in range(HEADS):
                    k = h + (HEADS if which == "wk" else 0)
                    pe.wait_ge(s_q2, K + k + 1)
                    nc.tensor.matmul(ps[0:96, QK + h, :], w(which)[:, 96 * h:96 * h + 96], xln[:, par, :],
                                     start=True, stop=True).then_inc(s_qk, 1)

            pe.wait_ge(s_cst, 16)
            pe.wait_ge(s_prep, 6)
            pe.sem_inc(s_pv, NB)
            for q in (s_proj, s_fc2, s_outp):
                pe.sem_inc(q, START)
            with pe.Fori(0, B) as b:
                pe.wait_ge(s_x, (b + 1) * 16)
                L0 = b * 2 * NCH
                mean(0, L0)
                var(0, L0)

                def qkv(i, par, more):
                    K = (b * NCH + i) * 2 * HEADS
                    if more:
                        mean(i + 1, L0 + i + 1)
                    pe.wait_ge(s_xln, L0 + i + 1)
                    project(par, K, "wq")
                    if more:
                        var(1 - par, L0 + i + 1)
                    project(par, K, "wk")
                    pe.wait_ge(s_vr, START + b * NCH + i)
                    for t in range(4):
                        mm = nc.tensor.matmul(ps[:, VB, 128 * t:128 * t + 128], xln[:, par, 128 * t:128 * t + 128],
                                              w("wv"), start=True, stop=True)
                    mm.then_inc(s_v, 1)
                chunks(pe, qkv)

                def max_tile(j, m, head):
                    pe.wait_ge(s_red, (b * NJ + j) * TILES + m + 1)
                    nc.tensor.matmul(ps[:, SM + m % 2, :], qst[0:96, ds(j * TC + m // NCH * 128, 128)],
                                     kst[0:96, ds(head + m % NCH * TC, TC)],
                                     start=True, stop=True).then_inc(s_sm, 1)

                def scores(j, u, head):
                    if not (isinstance(j, int) and j == 0 and u < 2):
                        pe.wait_ge(s_p32, (b * NJ + j) * UNITS + u - 1)
                    if u == 0:
                        pe.wait_ge(s_cdma, 32 * (b * NJ + j + 1))
                    for t in range(2):
                        mm = nc.tensor.matmul(ps[:, ST + 2 * (u % 2) + t, :],
                                              kst[0:98, ds(head + (2 * u + t) * 128, 128)],
                                              qst[0:98, ds(j * TC, TC)], start=True, stop=True)
                    mm.then_inc(s_st, 1)

                def pv(j, u, head):
                    J = b * NJ + j
                    if SUB[u] == "P":
                        pe.wait_ge(s_subp, J * SUB_P + upto(SUB, "P", u))
                    else:
                        pe.wait_ge(s_subd, J * SUB_D + upto(SUB, "D", u))
                    if u == 0:
                        pe.wait_ge(s_oev, START + J)
                    for t in range(2):
                        for n, part in enumerate((p1, p2)):
                            mm = nc.tensor.matmul(ps[:, OB, :], vst[:, ds(head + (2 * u + t) * 128, 128)],
                                                  part[:, u % NB, TC * t:TC * t + TC],
                                                  start=(u == 0 and t == 0 and n == 0),
                                                  stop=(u == UNITS - 1 and t == 1 and n == 1))
                    mm.then_inc(s_pv, 1)

                def turn_max(idx, J):
                    pe.wait_ge(s_cneg, J + 1)
                    pe.wait_ge(s_tbfree, b * 3 * NJ + idx + 1)
                    nc.tensor.transpose(ps[0:4, TB, 0:128], cneg[:, :], w("ident")).then_inc(s_ct, 1)

                def spread_sums(idx, J):
                    pe.wait_ge(s_rcp, J + 1)
                    pe.wait_ge(s_tbfree, b * 3 * NJ + idx + 1)
                    nc.tensor.matmul(ps[0:96, TB, :], w("spread")[96:128, 0:96], rcp[96:128, :],
                                     start=True, stop=True).then_inc(s_bc, 1)

                def out_project(idx, J):
                    pe.wait_ge(s_on, START + J + 1)
                    pe.wait_ge(s_pcur, J + 1)
                    pe.wait_ge(s_tbfree, b * 3 * NJ + idx + 1)
                    nc.tensor.matmul(ps[:, TB, :], pcur[:, :], onrm[:, :],
                                     start=True, stop=True).then_inc(s_proj, 1)

                pe.wait_ge(s_fill, 2 * b + 2)
                pe.wait_ge(s_q2, 4 + (b + 1) * NCH * 2 * HEADS)
                for m in range(TILES):
                    max_tile(0, m, 0)
                turn_max(0, b * NJ)
                for m in range(TILES):
                    max_tile(1, m, 0)
                pe.wait_ge(s_v3, START + (b + 1) * NCH)
                for u in range(LAG):
                    scores(0, u, 0)

                def attend(j, first, has_next, has_max):
                    J = b * NJ + j
                    base = 2 + 3 * (j - 1) if not first else 1
                    for u in range(UNITS):
                        if u + LAG < UNITS:
                            scores(j, u + LAG, head_base(j))
                        elif has_next:
                            scores(j + 1, u + LAG - UNITS, head_base(j + 1))
                        if has_max:
                            for m in (2 * u, 2 * u + 1):
                                max_tile(j + 2, m, head_base(j + 2))
                        pv(j, u, head_base(j))
                        if u == 1 and has_next:
                            turn_max(base, J + 1)
                        if u == 4 and not first:
                            spread_sums(base + has_next, J - 1)
                        if u == 8 and not first:
                            out_project(base + has_next + 1, J - 1)
                qchunks(pe, attend)
                spread_sums(3 * NJ - 2, b * NJ + NJ - 1)
                out_project(3 * NJ - 1, b * NJ + NJ - 1)

                pe.wait_ge(s_tbfree, 1 + (b + 1) * 3 * NJ)
                mean(0, L0 + NCH)
                var(0, L0 + NCH)

                def mlp(i, par, more):
                    L = L0 + NCH + i
                    G = b * NCH + i
                    if more:
                        mean(i + 1, L + 1)
                    pe.wait_ge(s_xln, L + 1)
                    pe.wait_ge(s_gelu, START + 2 * G)
                    for n in range(2):
                        nc.tensor.matmul(ps[:, FC1 + n, :], w("w1")[:, 128 * n:128 * n + 128], xln[:, par, :],
                                         start=True, stop=True).then_inc(s_fc1, 1)
                    if more:
                        var(1 - par, L + 1)
                    pe.wait_ge(s_gelu, START + 2 * G + 2)
                    pe.wait_ge(s_x2, START + G)
                    for n in range(2):
                        mm = nc.tensor.matmul(ps[:, FC2, :], w("w2")[:, 128 * n:128 * n + 128], hid[:, n, :],
                                              start=(n == 0), stop=(n == 1))
                    mm.then_inc(s_fc2, 1)
                chunks(pe, mlp)

                Q0 = b * NQ

                def conv(f):
                    if not isinstance(f, int):
                        pe.wait_ge(s_xr, START + Q0 + f - 3)
                    if not (isinstance(f, int) and f == 0):
                        pe.wait_ge(s_dt, Q0 + f)
                    for n in range(9):
                        rows = x2[:, ds(4 * f + n // 3, 4), n % 3:n % 3 + SIDE]
                        mm = nc.tensor.matmul(ps[:, SA, 0:SEQ].rearrange("p (r w) -> p r w", r=4),
                                              w("conv")[:, 128 * n:128 * n + 128], rows,
                                              start=(n == 0), stop=(n == 8))
                    mm.then_inc(s_conv, 1)

                def turn(f):
                    pe.wait_ge(s_yc, Q0 + f + 1)
                    if not (isinstance(f, int) and f == 0):
                        pe.wait_ge(s_rbc, Q0 + f)
                    for r in range(2):
                        mm = nc.tensor.transpose(ps[:, SB, C * r:C * r + C], yc[:, C * r:C * r + C], w("ident"))
                    mm.then_inc(s_tr, 1)

                def in_project(f):
                    pe.wait_ge(s_yT, Q0 + f + 1)
                    for k, bank, s_k in (("xi", SA, s_xi), ("z", SB, s_zz)):
                        for n in range(2):
                            mm = nc.tensor.matmul(ps[:, bank, SEQ * n:SEQ * n + SEQ],
                                                  w(k)[:, 128 * n:128 * n + 128], yT[:, :], start=True, stop=True)
                        mm.then_inc(s_k, 1)

                def x_project(f):
                    pe.wait_ge(s_xcs, Q0 + f + 1)
                    pe.wait_ge(s_szs, Q0 + f + 1)
                    nc.tensor.matmul(ps[:, SA, :], w("dt"), slot(xcs, f), start=True, stop=True).then_inc(s_dtp, 1)
                    nc.tensor.matmul(ps[:, SB, :], w("bc"), slot(xcs, f), start=True, stop=True).then_inc(s_bcp, 1)

                def spread_bc(q, first):
                    Q = Q0 + q
                    pe.wait_ge(s_sbc, 16 * 12 * (Q + 1))
                    for n in range(8):
                        k = n % 4
                        if n == 0 and not first:
                            pe.wait_ge(s_da, Q * 16)
                        if n == 2 and not first:
                            pe.wait_ge(s_dbx, Q * 16)
                        if n >= 4:
                            pe.wait_ge(s_bcev, Q * 8 + n - 3)
                        sel = spread[0:96, 512 + 128 * (n // 4):640 + 128 * (n // 4)]
                        nc.tensor.matmul(ps[:, k, :], sel, stack("bc", q, k), start=True, stop=True).then_inc(s_bcu, 1)

                def spread_group(q, g):
                    Q = Q0 + q
                    sel = spread[0:96, 128 * g:128 * g + 128]
                    if g == 0:
                        pe.wait_ge(s_sdt, 16 * 12 * (Q + 1))
                        pe.wait_ge(s_su, 16 * 12 * (Q + 1))
                    for k in range(4):
                        n = Q * 16 + g * 4 + k
                        if g == 0 and k < 2:
                            pe.wait_ge(s_bcev, Q * 8 + 5 + k)
                        else:
                            pe.wait_ge(s_da, n - 1)
                        nc.tensor.matmul(ps[:, DT + k % 2, :], sel, stack("dt", q, k),
                                         start=True, stop=True).then_inc(s_dtu, 1)
                        if g == 0 and k < 2:
                            pe.wait_ge(s_bcev, Q * 8 + 7 + k)
                        else:
                            pe.wait_ge(s_dbx, n - 1)
                        nc.tensor.matmul(ps[:, UU + k % 2, :], sel, stack("u", q, k),
                                         start=True, stop=True).then_inc(s_uu, 1)

                def sum_states(q, g, first):
                    Q = Q0 + q
                    wait_hc(pe, Q, g)
                    if g == 0 and not first:
                        pe.wait_ge(s_ya, Q)
                    for t in range(L):
                        r = 32 * (t % 4)
                        mm = nc.tensor.matmul(ps[r:r + 32, YB + t // 4, 0:SEQ], w("sum")[:, 32 * g:32 * g + 32],
                                              hC[:, g % 2, SEQ * t:SEQ * t + SEQ],
                                              start=(g == 0), stop=(g == GR - 1))
                    mm.then_inc(s_y, 1)

                def out_project(q, fronts):
                    pe.wait_ge(s_ym, START + Q0 + q + 1)
                    pe.wait_ge(s_dt, Q0 + fronts)
                    pe.wait_ge(s_xr, START + Q0 + q)
                    for r in range(2):
                        for n in range(2):
                            mm = nc.tensor.matmul(ps[:, SA, 128 * r + 64 * n:128 * r + 64 * n + 64],
                                                  ym[:, SEQ * n + C * r:SEQ * n + C * r + C], w("out"),
                                                  start=True, stop=True)
                    mm.then_inc(s_outp, 1)

                pe.wait_ge(s_x2, START + (b + 1) * NCH)
                for f in range(2):
                    conv(f)
                    turn(f)
                    in_project(f)
                    x_project(f)

                def scan_chunk(q, first, has_front):
                    spread_bc(q, first)
                    spread_group(q, 0)
                    if has_front:
                        conv(q + 2)
                    spread_group(q, 1)
                    if has_front:
                        turn(q + 2)
                    sum_states(q, 0, first)
                    if has_front:
                        in_project(q + 2)
                    spread_group(q, 2)
                    if has_front:
                        x_project(q + 2)
                    sum_states(q, 1, first)
                    spread_group(q, 3)
                    sum_states(q, 2, first)
                    if not first:
                        out_project(q - 1, q + 3 if has_front else NQ)
                    sum_states(q, 3, first)
                mchunks(pe, scan_chunk)
                out_project(NQ - 1, NQ)

                pe.wait_ge(s_gsum, b + 1)
                nc.tensor.matmul(ps[:, SB, 0:1], w("group"), gs[:, 0:1], start=True, stop=True).then_inc(s_gmm, 1)
                pe.wait_ge(s_gsq, b + 1)
                nc.tensor.matmul(ps[:, SB, 0:1], w("group"), gs[:, 2:3], start=True, stop=True).then_inc(s_gvv, 1)

        @block.scalar
        def _(act):
            def square(par, L):
                act.wait_ge(s_xc, START + L + 1)
                nc.scalar.activation(sq[:, par, :], xc[:, par, :], ACT.Square).then_inc(s_sq, 1)

            def inverse_deviation(par, L):
                act.wait_ge(s_var, L + 1)
                nc.scalar.activation(lnv[:, :], ps[:, VAR, :], ACT.Ln, bias=vec("eps")).then_inc(s_ln, 1)
                act.wait_ge(s_ln, START + L + 1)
                nc.scalar.activation(rstd[:, par, :], lnv[:, :], ACT.Exp, scale=-0.5).then_inc(s_rstd, 1)

            act.wait_ge(s_cst, 16)
            for q in (s_ln, s_oev, s_gelu, s_xr):
                act.sem_inc(q, START)
            act.wait_ge(s_raw, 16)
            nc.scalar.activation(spread[0:96, :], raw[0:96, raw_at["spread_e"]:raw_at["spread_e"] + 768],
                                 ACT.Copy).then_inc(s_prep, 1)
            nc.scalar.activation(negA[:, :], w("A"), ACT.Exp).then_inc(s_prep, 1)
            act.wait_ge(s_prep, 6)
            with act.Fori(0, B) as b:
                L0 = b * 2 * NCH
                square(0, L0)
                inverse_deviation(0, L0)

                def qkv(i, par, more):
                    L = L0 + i
                    K = (b * NCH + i) * 2 * HEADS
                    if more:
                        square(1 - par, L + 1)
                    for k in range(2 * HEADS):
                        if k == HEADS and more:
                            inverse_deviation(1 - par, L + 1)
                        act.wait_ge(s_qk, K + k + 1)
                        st = qst if k < HEADS else kst
                        h = k % HEADS
                        nc.scalar.activation(st[0:96, ds(i * TC + h * N, TC)], ps[0:96, QK + h, :],
                                             ACT.Copy, scale=QS).then_inc(s_q1, 1)
                    act.wait_ge(s_v, b * NCH + i + 1)
                    nc.scalar.activation(v_part(0, i), v_psum(), ACT.Copy).then_inc(s_v1, 1)
                chunks(act, qkv)

                def attend(j, first, has_next, has_max):
                    J = b * NJ + j
                    for u in range(UNITS):
                        n = J * UNITS + u
                        act.wait_ge(s_st, n + 1)
                        act.wait_ge(s_pv, n + 1)
                        src = ps[:, ST + 2 * (u % 2):ST + 2 * (u % 2) + 2, :]
                        if CAST[u] == "A":
                            nc.scalar.activation(p1[:, u % NB, :], src, ACT.Exp, scale=SCALE)
                        nc.scalar.activation(p32[:, u % NB, :], src, ACT.Exp, scale=SCALE).then_inc(s_p32, 1)
                        if u == 1 and not first:
                            read_sums(J - 1)

                def read_sums(J):
                    act.wait_ge(s_pv, NB + (J + 1) * UNITS)
                    act.wait_ge(s_on, START + J)
                    nc.scalar.activation(osb[:, :], ps[:, OB, :], ACT.Copy).then_inc(s_oev, 1)
                    act.wait_ge(s_oev, START + J + 1)
                    nc.scalar.activation(lns[96:128, :], osb[96:128, :], ACT.Ln).then_inc(s_lns, 1)
                    act.wait_ge(s_lns, J + 1)
                    nc.scalar.activation(rcp[96:128, :], lns[96:128, :], ACT.Exp, scale=-1.0).then_inc(s_rcp, 1)
                qchunks(act, attend)
                read_sums(b * NJ + NJ - 1)

                square(0, L0 + NCH)
                inverse_deviation(0, L0 + NCH)

                def mlp(i, par, more):
                    L = L0 + NCH + i
                    G = b * NCH + i
                    if more:
                        square(1 - par, L + 1)
                    for n in range(2):
                        act.wait_ge(s_fc1, 2 * G + n + 1)
                        if n == 0:
                            act.wait_ge(s_fc2, START + G)
                        nc.scalar.activation(hid[:, n, :], ps[:, FC1 + n, :], ACT.Gelu,
                                             bias=vec(f"fc1_b{n}")).then_inc(s_gelu, 1)
                    if more:
                        inverse_deviation(1 - par, L + 1)
                chunks(act, mlp)

                Q0 = b * NQ

                def front_a(f):
                    act.wait_ge(s_conv, Q0 + f + 1)
                    nc.scalar.activation(yc[:, :], ps[:, SA, 0:SEQ], ACT.Identity, bias=vec("conv_b")).then_inc(s_yc, 1)

                def front_b(f):
                    act.wait_ge(s_tr, Q0 + f + 1)
                    nc.scalar.activation(yT[:, :], ps[:, SB, 0:SEQ], ACT.Copy).then_inc(s_yT, 1)
                    act.wait_ge(s_xi, Q0 + f + 1)
                    if not isinstance(f, int):
                        act.wait_ge(s_ym, START + Q0 + f - 3)
                    nc.scalar.activation(slot(xcs, f), ps[:, SA, :], ACT.Silu, bias=vec("conv1d_b")).then_inc(s_xcs, 1)
                    act.wait_ge(s_zz, Q0 + f + 1)
                    nc.scalar.activation(slot(szs, f), ps[:, SB, :], ACT.Silu).then_inc(s_szs, 1)

                def front_c(f):
                    act.wait_ge(s_bcp, Q0 + f + 1)
                    if not (isinstance(f, int) and f == 0):
                        act.wait_ge(s_sbc, 16 * 12 * (Q0 + f))
                    nc.scalar.activation(pcs["bc"][:, 0, :], ps[:, SB, :], ACT.Copy).then_inc(s_bc1, 1)

                def front_s(f):
                    act.wait_ge(s_m, Q0 + f + 1)
                    nc.scalar.activation(edt[:, :], mdt[:, :], ACT.Exp).then_inc(s_e, 1)
                    act.wait_ge(s_e, Q0 + f + 1)
                    nc.scalar.activation(ldt[:, :], edt[:, :], ACT.Ln, bias=1.0).then_inc(s_l, 1)

                def spread_bc(q, first):
                    Q = Q0 + q
                    for n in range(8):
                        if n == 0 and not first:
                            act.wait_ge(s_dbx, Q * 16)
                        if n == 4 and not first:
                            wait_hc(act, Q - 1, GR - 1)
                            wait_hc(act, Q - 1, GR - 2)
                        act.wait_ge(s_bcu, Q * 8 + n + 1)
                        dst = (bsb if n < 4 else csb)[:, TC * (n % 4):TC * (n % 4) + TC]
                        nc.scalar.activation(dst, ps[:, n % 4, :], ACT.Copy).then_inc(s_bcev, 1)

                def decays(q, g, first):
                    Q = Q0 + q
                    if not (first and g < 2):
                        act.wait_ge(s_scan, Q * GR + g - 1)
                    for k in range(4):
                        act.wait_ge(s_dtu, Q * 16 + g * 4 + k + 1)
                        lo = 1 if k == 0 else 0
                        src = ps[:, DT + k % 2, :].rearrange("p (t n) -> p t n", t=2)[:, lo:2, :]
                        nc.scalar.activation(tn(dA[:, g % 2, :], k)[:, lo:2, :], src, ACT.Exp,
                                             scale=negA[:, g:g + 1]).then_inc(s_da, 1)

                def out_rows(q):
                    act.wait_ge(s_outp, START + Q0 + q + 1)
                    nc.scalar.activation(xr[:, ds(q * SEQ, SEQ)], ps[:, SA, 0:SEQ], ACT.Copy).then_inc(s_xr, 1)

                for f in range(2):
                    front_a(f)
                    front_b(f)
                    front_c(f)
                    front_s(f)

                def scan_chunk(q, first, has_front):
                    spread_bc(q, first)
                    decays(q, 0, first)
                    if has_front:
                        front_a(q + 2)
                    decays(q, 1, first)
                    if has_front:
                        front_b(q + 2)
                    decays(q, 2, first)
                    if has_front:
                        front_c(q + 2)
                    decays(q, 3, first)
                    if has_front:
                        front_s(q + 2)
                    if not first:
                        out_rows(q - 1)
                mchunks(act, scan_chunk)
                out_rows(NQ - 1)

                act.wait_ge(s_xr, START + Q0 + NQ)
                nc.scalar.activation(junk[:, :], xr[:, :], ACT.Copy, accum_out=gs[:, 0:1]).then_inc(s_gsum, 1)
                act.wait_ge(s_gmu, b + 1)
                nc.scalar.activation(junk[:, :], xr[:, :], ACT.Square, bias=gs[:, 1:2],
                                     accum_out=gs[:, 2:3]).then_inc(s_gsq, 1)
                act.wait_ge(s_gvv, b + 1)
                nc.scalar.activation(gs[:, 3:4], ps[:, SB, 0:1], ACT.Ln, bias=vec("eps")).then_inc(s_gln, 1)
                act.wait_ge(s_gln, b + 1)
                nc.scalar.activation(gs[:, 4:5], gs[:, 3:4], ACT.Exp, scale=-0.5).then_inc(s_grs, 1)
                act.wait_ge(s_gsc, b + 1)
                for n in range(4):
                    nc.scalar.activation(xp[:, 1024 * n:1024 * n + 1024], xr[:, 1024 * n:1024 * n + 1024], ACT.Silu,
                                         scale=gs[:, 5:6], bias=gs[:, 6:7]).then_inc(s_gxp, 1)

        @block.vector
        def _(dve):
            def centre(i, par, L):
                dve.wait_ge(s_mean, L + 1)
                nc.vector.tensor_tensor(xc[:, par, :], x[:, ds(i * TC, TC)], ps[:, MEAN, :],
                                        ALU.subtract).then_inc(s_xc, 1)

            def normalise(par, L):
                dve.wait_ge(s_rstd, L + 1)
                nc.vector.tensor_tensor(z[:, par, :], xc[:, par, :], rstd[:, par, :], ALU.mult).then_inc(s_z, 1)

            dve.sem_inc(s_q2, 4)
            dve.sem_inc(s_red, 2)
            dve.sem_inc(s_tbfree, 1)
            for q in (s_xc, s_vr, s_on, s_x2, s_ym):
                dve.sem_inc(q, START)
            dve.wait_ge(s_cst, 16)
            dve.wait_ge(s_raw, 16)
            r = lambda k: raw[:, raw_at[k]:raw_at[k] + RAW[k]]
            nc.vector.memset(x2[:, :, :], 0.0).then_inc(s_prep, 1)
            nc.vector.tensor_tensor(w("xi"), w("xi"), r("conv1d"), ALU.mult).then_inc(s_prep, 1)
            nc.vector.tensor_tensor(w("dt"), w("dt"), r("dt_row"), ALU.mult).then_inc(s_prep, 1)
            dve.wait_ge(s_prep, 5)
            nc.vector.tensor_scalar(negA[:, :], negA[:, :], -1.0, None, ALU.mult).then_inc(s_prep, 1)
            dve.wait_ge(s_prep, 6)
            with dve.Fori(0, B) as b:
                L0 = b * 2 * NCH
                centre(0, 0, L0)
                normalise(0, L0)

                def qkv(i, par, more):
                    L = L0 + i
                    K = (b * NCH + i) * 2 * HEADS
                    if more:
                        centre(i + 1, 1 - par, L + 1)
                    for k in range(2 * HEADS):
                        if k == HEADS and more:
                            normalise(1 - par, L + 1)
                        dve.wait_ge(s_q1, K + k + 1)
                        st, r = (qst, 64) if k < HEADS else (kst, 32)
                        h = k % HEADS
                        low = st[r:r + 32, ds(i * TC + h * N, TC)]
                        nc.vector.scalar_tensor_tensor(out=low, in0=ps[r:r + 32, QK + h, :], scalar=QS, in1=low,
                                                       op0=ALU.mult, op1=ALU.subtract).then_inc(s_q2, 1)
                    dve.wait_ge(s_v1, b * NCH + i + 1)
                    dve.wait_ge(s_v3, START + b * NCH + i)
                    nc.vector.tensor_tensor(vres4(), v_psum(), v_part(0, i), ALU.subtract).then_inc(s_vr, 1)
                chunks(dve, qkv)

                def reduce_tile(j, m):
                    T = (b * NJ + j) * TILES + m
                    dve.wait_ge(s_sm, T + 1)
                    nc.vector.tensor_reduce(mx[:, m:m + 1], ps[:, SM + m % 2, :], AX.X,
                                            ALU.max).then_inc(s_red, 1)

                def chunk_max(J):
                    dve.wait_ge(s_red, 2 + (J + 1) * TILES)
                    nc.vector.tensor_reduce(cneg[:, :], mx[:, :].rearrange("p (q t) -> p q t", q=4), AX.X,
                                            ALU.max, negate=True).then_inc(s_cneg, 1)

                def max_rows(J, first=False):
                    dve.wait_ge(s_ct, J + 1)
                    nc.vector.tensor_scalar(crow[:, :], ps[0:4, TB, 0:128], 1.0 / ROW, SHIFT,
                                            ALU.mult, ALU.add).then_inc(s_tbfree, 1)
                    if not first:
                        dve.wait_ge(s_cdma, 32 * J)
                    dve.wait_ge(s_tbfree, tb[0] + 1)
                    tb[0] = tb[0] + 1
                    nc.vector.tensor_copy(chi[:, :], crow[:, :]).then_inc(s_chi, 1)
                    dve.wait_ge(s_chi, J + 1)
                    nc.vector.tensor_tensor(clo[:, :], crow[:, :], chi[:, :], ALU.subtract).then_inc(s_clo, 1)

                def parts(j, u):
                    n = (b * NJ + j) * UNITS + u
                    J = b * NJ + j
                    if CAST[u] == "D":
                        dve.wait_ge(s_p32, n + 1)
                        nc.vector.tensor_copy(p1[:, u % NB, :], p32[:, u % NB, :]).then_inc(s_p1d, 1)
                        if SUB[u] == "D":
                            dve.wait_ge(s_p1d, J * CAST_D + upto(CAST, "D", u))
                    if SUB[u] == "D":
                        if CAST[u] != "D":
                            dve.wait_ge(s_p32, n + 1)
                        nc.vector.tensor_tensor(p2[:, u % NB, :], p32[:, u % NB, :], p1[:, u % NB, :],
                                                ALU.subtract).then_inc(s_subd, 1)

                def scale_sums(J):
                    dve.wait_ge(s_bc, J + 1)
                    nc.vector.tensor_tensor(onrm[:, :], osb[0:96, :], ps[0:96, TB, :],
                                            ALU.mult).then_inc(s_on, 1)
                    dve.wait_ge(s_on, START + J + 1)
                    dve.sem_inc(s_tbfree, 1)

                def add_heads(j, J):
                    dve.wait_ge(s_proj, START + J + 1)
                    xs = x[:, ds((j & (NCH - 1)) * TC, TC)]
                    nc.vector.scalar_tensor_tensor(out=xs, in0=ps[:, TB, :], scalar=w("head_bias")[:, ds(j // NCH, 1)], in1=xs,
                                                   op0=ALU.add, op1=ALU.add).then_inc(s_tbfree, 1)

                tb = [None]
                for m in range(TILES):
                    reduce_tile(0, m)
                chunk_max(b * NJ)
                tb[0] = 1 + b * 3 * NJ
                max_rows(b * NJ, True)
                dve.wait_ge(s_cneg, b * NJ + 1)
                for m in range(TILES):
                    reduce_tile(1, m)
                parts(0, 0)

                def attend(j, first, has_next, has_max):
                    J = b * NJ + j
                    tb[0] = 1 + b * 3 * NJ + (1 if first else 2 + 3 * (j - 1))
                    if has_next:
                        chunk_max(J + 1)
                        dve.wait_ge(s_cneg, J + 2)
                    for u in range(UNITS):
                        if has_max:
                            reduce_tile(j + 2, 2 * u)
                            reduce_tile(j + 2, 2 * u + 1)
                        if u + 1 < UNITS:
                            parts(j, u + 1)
                        elif has_next:
                            parts(j + 1, 0)
                        if u == 2 and has_next:
                            max_rows(J + 1)
                        if u == 5 and not first:
                            scale_sums(J - 1)
                        if u == 9 and not first:
                            add_heads(j - 1, J - 1)
                qchunks(dve, attend)
                scale_sums(b * NJ + NJ - 1)
                add_heads(NJ - 1, b * NJ + NJ - 1)

                centre(0, 0, L0 + NCH)
                normalise(0, L0 + NCH)

                def mlp(i, par, more):
                    L = L0 + NCH + i
                    G = b * NCH + i
                    if more:
                        centre(i + 1, 1 - par, L + 1)
                        normalise(1 - par, L + 1)
                    dve.wait_ge(s_fc2, START + G + 1)
                    nc.vector.scalar_tensor_tensor(
                        out=x2[:, ds(i * ROWS + 1, ROWS), 1:SIDE + 1],
                        in0=ps[:, FC2, :].rearrange("p (r w) -> p r w", r=ROWS), scalar=vec("fc2_b"),
                        in1=x[:, ds(i * TC, TC)].rearrange("p (r w) -> p r w", r=ROWS),
                        op0=ALU.add, op1=ALU.add).then_inc(s_x2, 1)
                chunks(dve, mlp)

                Q0 = b * NQ

                def front_d(f):
                    FQ = Q0 + f
                    dve.wait_ge(s_dtp, FQ + 1)
                    nc.vector.tensor_scalar(mdt[:, :], ps[:, SA, :], vec("dt_b"), 30.0, ALU.add,
                                            ALU.min).then_inc(s_m, 1)
                    dve.wait_ge(s_bc1, FQ + 1)
                    nc.vector.tensor_tensor(rbc[:, :], ps[:, SB, :], pcs["bc"][:, 0, :],
                                            ALU.subtract).then_inc(s_rbc, 1)

                def front_e(f):
                    FQ = Q0 + f
                    c = [FQ * 8]

                    def link(ins):
                        ins.then_inc(s_chain, 1)
                        c[0] = c[0] + 1
                        dve.wait_ge(s_chain, c[0])
                    dve.wait_ge(s_l, FQ + 1)
                    nc.vector.scalar_tensor_tensor(out=dts[:, :], in0=ps[:, SA, :], scalar=vec("dt_b"), in1=ldt[:, :],
                                                   op0=ALU.add, op1=ALU.max).then_inc(s_dt, 1)
                    dve.wait_ge(s_dt, FQ + 1)
                    dve.wait_ge(s_xcs, FQ + 1)
                    link(nc.vector.tensor_tensor(us[:, :], dts[:, :], slot(xcs, f), ALU.mult))
                    if not (isinstance(f, int) and f == 0):
                        dve.wait_ge(s_sdt, 16 * 12 * FQ)
                        dve.wait_ge(s_su, 16 * 12 * FQ)
                    dve.wait_ge(s_rbc, FQ + 1)
                    nc.vector.tensor_copy(pcs["bc"][:, 1, :], rbc[:, :])
                    nc.vector.tensor_copy(pcs["dt"][:, 0, :], dts[:, :])
                    link(nc.vector.tensor_copy(pcs["u"][:, 0, :], us[:, :]))
                    nc.vector.tensor_tensor(rdt[:, :], dts[:, :], pcs["dt"][:, 0, :], ALU.subtract)
                    nc.vector.tensor_tensor(ru[:, :], us[:, :], pcs["u"][:, 0, :], ALU.subtract)
                    link(nc.vector.tensor_tensor(pcs["bc"][:, 2, :], rbc[:, :], pcs["bc"][:, 1, :], ALU.subtract))
                    nc.vector.tensor_copy(pcs["dt"][:, 1, :], rdt[:, :])
                    link(nc.vector.tensor_copy(pcs["u"][:, 1, :], ru[:, :]))
                    nc.vector.tensor_tensor(pcs["dt"][:, 2, :], rdt[:, :], pcs["dt"][:, 1, :], ALU.subtract)
                    nc.vector.tensor_tensor(pcs["u"][:, 2, :], ru[:, :], pcs["u"][:, 1, :],
                                            ALU.subtract).then_inc(s_pcs, 1)
                    dve.sem_inc(s_chain, 4)

                def scan_group(q, g, first):
                    Q = Q0 + q
                    for k in range(4):
                        dve.wait_ge(s_uu, Q * 16 + g * 4 + k + 1)
                        if g == 0:
                            dve.wait_ge(s_bcev, Q * 8 + k + 1)
                        u2 = ps[:, UU + k % 2, :].rearrange("p (t n) -> p t n", t=2)
                        b2 = bsb[:, TC * k:TC * k + TC].rearrange("p (t n) -> p t n", t=2)
                        nc.vector.tensor_tensor(tn(dbx[:, g % 2, :], k), u2, b2, ALU.mult).then_inc(s_dbx, 1)
                    dve.wait_ge(s_dbx, Q * 16 + g * 4 + 4)
                    dve.wait_ge(s_da, Q * 16 + g * 4 + 4)
                    if g == 0 and first:
                        dve.wait_ge(s_dz, b + 1)
                    elif g == 0:
                        wait_hc(dve, Q - 1, GR - 1)
                    else:
                        wait_hc(dve, Q, g - 1)
                    nc.vector.tensor_tensor_scan(hs[:, :], dA[:, g % 2, :], dbx[:, g % 2, :], 0.0, ALU.mult,
                                                 ALU.add).then_inc(s_scan, 1)
                    if g in HC_DVE:
                        times_c(dve, nc.vector, Q, g, first, s_hcd)

                def gate(q):
                    Q = Q0 + q
                    dve.wait_ge(s_y, (Q + 1) * GR)
                    nc.vector.scalar_tensor_tensor(
                        out=ya[:, :].rearrange("p (h n) -> p h n", h=2), in0=slot(xcs, q).rearrange("p (h n) -> p h n", h=2),
                        scalar=vec("D"), in1=ps[:, YB:YB + 2, 0:SEQ], op0=ALU.mult, op1=ALU.add).then_inc(s_ya, 1)
                    dve.wait_ge(s_ya, Q + 1)
                    dve.wait_ge(s_outp, START + Q)
                    nc.vector.tensor_tensor(ym[:, :], ya[:, :], slot(szs, q), ALU.mult).then_inc(s_ym, 1)

                for f in range(2):
                    front_d(f)
                    front_e(f)

                def scan_chunk(q, first, has_front):
                    scan_group(q, 0, first)
                    if not first:
                        gate(q - 1)
                    scan_group(q, 1, first)
                    scan_group(q, 2, first)
                    if has_front:
                        front_d(q + 2)
                    scan_group(q, 3, first)
                    if has_front:
                        front_e(q + 2)
                mchunks(dve, scan_chunk)
                gate(NQ - 1)

                dve.wait_ge(s_gmm, b + 1)
                nc.vector.tensor_scalar(gs[:, 1:2], ps[:, SB, 0:1], -1.0, None, ALU.mult).then_inc(s_gmu, 1)
                dve.wait_ge(s_grs, b + 1)
                nc.vector.tensor_scalar(gs[:, 5:6], gs[:, 4:5], vec("gn_w"), None, ALU.mult).then_inc(s_gsc2, 1)
                dve.wait_ge(s_gsc2, b + 1)
                nc.vector.scalar_tensor_tensor(out=gs[:, 6:7], in0=gs[:, 1:2], scalar=gs[:, 5:6], in1=vec("gn_b"),
                                               op0=ALU.mult, op1=ALU.add).then_inc(s_gsc, 1)
                for n in range(4):
                    dve.wait_ge(s_gxp, b * 4 + n + 1)
                    rows = fin[:, 1024 * n:1024 * n + 1024].rearrange("p (r w) -> p r w", r=16)
                    nc.vector.tensor_tensor(rows, xp[:, 1024 * n:1024 * n + 1024].rearrange("p (r w) -> p r w", r=16),
                                            x2[:, 16 * n + 1:16 * n + 17, 1:SIDE + 1], ALU.add).then_inc(s_fin, 1)

        @block.gpsimd
        def _(pool):
            def affine(par, L, norm):
                pool.wait_ge(s_z, L + 1)
                pool.sem_inc(s_seen, 1)
                nc.gpsimd.tensor_scalar(xln[:, par, :], z[:, par, :], vec(f"ln{norm}_w"), vec(f"ln{norm}_b"),
                                        ALU.mult, ALU.add).then_inc(s_xln, 1)
            pool.sem_inc(s_v3, START)
            pool.wait_ge(s_cst, 16)
            with pool.Fori(0, B) as b:
                L0 = b * 2 * NCH
                pool.wait_ge(s_prep, 6)
                pool.wait_ge(s_x, 16 * (b + 1))
                pool.sem_inc(s_seen, 1)
                nc.gpsimd.memset(kst[96:128, :], ROW).then_inc(s_fill, 1)
                pool.wait_ge(s_fill, 2 * b + 1)
                pool.sem_inc(s_seen, 1)
                nc.gpsimd.memset(vst[:, :].rearrange("p (n m) -> p n m", m=128)[:, :, 96:128],
                                 1.0).then_inc(s_fill, 1)
                pool.wait_ge(s_fill, 2 * b + 2)
                affine(0, L0, 1)

                def qkv(i, par, more):
                    G = b * NCH + i
                    if more:
                        affine(1 - par, L0 + i + 1, 1)
                    pool.wait_ge(s_vr, START + G + 1)
                    pool.sem_inc(s_seen, 1)
                    nc.gpsimd.tensor_copy(v_part(1, i), vres4()).then_inc(s_v2, 1)
                    pool.wait_ge(s_v2, G + 1)
                    nc.gpsimd.tensor_tensor(v_part(2, i), vres4(), v_part(1, i), ALU.subtract).then_inc(s_v3, 1)
                chunks(pool, qkv)

                def weights(j, J):
                    pool.wait_ge(s_proj, START + J)
                    pool.sem_inc(s_seen, 1)
                    nc.gpsimd.tensor_copy(pcur[:, :], w("proj")[0:96, ds((j & (NJ - NCH)) * (128 // NCH), 128)]).then_inc(s_pcur, 1)

                def attend(j, first, has_next, has_max):
                    J = b * NJ + j
                    for u in range(UNITS):
                        if u == 1 and not first:
                            weights(j - 1, J - 1)
                        if SUB[u] == "P":
                            if CAST[u] == "D":
                                pool.wait_ge(s_p1d, J * CAST_D + upto(CAST, "D", u))
                            else:
                                pool.wait_ge(s_p32, J * UNITS + u + 1)
                            nc.gpsimd.tensor_tensor(p2[:, u % NB, :], p32[:, u % NB, :], p1[:, u % NB, :],
                                                    ALU.subtract).then_inc(s_subp, 1)
                qchunks(pool, attend)
                weights(NJ - 1, b * NJ + NJ - 1)
                affine(0, L0 + NCH, 2)

                def mlp(i, par, more):
                    if more:
                        affine(1 - par, L0 + NCH + i + 1, 2)
                chunks(pool, mlp)

                pool.wait_ge(s_x2, START + (b + 1) * NCH)
                pool.sem_inc(s_seen, 1)
                nc.gpsimd.memset(dA[:, :, :].rearrange("p a (n t) -> p (a n) t", t=L)[:, :, 0:1], 0.0).then_inc(s_dz, 1)

                def scan_chunk(q, first, has_front):
                    for g in range(GR):
                        if g not in HC_DVE:
                            times_c(pool, nc.gpsimd, b * NQ + q, g, first, s_hcp)
                mchunks(pool, scan_chunk)

        @block.sync
        def _(sp):
            sp.dma_start(cst[:, :], consts_in).then_inc(s_cst, 16)
            sp.dma_start(raw[:, :], raw_in).then_inc(s_raw, 16)
            sp.dma_start(x[:, :], x_in[0].rearrange("c h w -> c (h w)")).then_inc(s_x, 16)

            def send_rows(j, J):
                sp.wait_ge(s_clo, J + 1)
                sp.sem_inc(s_step, 1)
                for n, part in enumerate((chi, clo)):
                    dst = qst[96 + n:97 + n, ds(j * TC, TC)]
                    sp.dma_start(dst, part[:, :]).then_inc(s_cdma, 16)

            def send_parts(f, Q0):
                FQ = Q0 + f
                sp.wait_ge(s_pcs, FQ + 1)
                if not (isinstance(f, int) and f < 2):
                    sp.wait_ge(s_uu, (FQ - 1) * 16)
                sp.sem_inc(s_step, 1)
                for k, s_k in (("bc", s_sbc), ("dt", s_sdt), ("u", s_su)):
                    to = stk[k].rearrange("p a b -> p (a b)")
                    for part in range(PARTS):
                        for t in range(4):
                            dst = to[32 * part:32 * part + 32, ds((f & 1) * COLS, COLS)]
                            dst = dst.rearrange("p (h t n) -> p h t n", h=2, t=4)[:, :, t, :]
                            src = pcs[k][32 * t:32 * t + 32, part, :].rearrange("p (h n) -> p h n", h=2)
                            sp.dma_start(dst, src).then_inc(s_k, 16)

            def image(b, last):
                send_rows(0, b * NJ)
                with sp.Fori(1, NJ) as j:
                    send_rows(j, b * NJ + j)
                send_parts(0, b * NQ)
                send_parts(1, b * NQ)
                with sp.Fori(2, NQ) as f:
                    send_parts(f, b * NQ)
                for n in range(4):
                    sp.wait_ge(s_fin, 4 * b + n + 1)
                    sp.sem_inc(s_step, 1)
                    sp.dma_start(out[ds(b, 1), :, 16 * n:16 * n + 16, :].rearrange("a c h w -> c (a h w)"),
                                 fin[:, 1024 * n:1024 * n + 1024]).then_inc(s_out, 16)
                sp.wait_ge(s_out, 64 * (b + 1))
                sp.sem_inc(s_step, 1)
                if not last:
                    sp.dma_start(x[:, :], x_in[ds(b + 1, 1)].rearrange("a c h w -> c (a h w)")).then_inc(s_x, 16)
            if B > 1:
                with sp.Fori(0, B - 1) as b:
                    image(b, False)
            image(B - 1, True)


def layout(inp):
    g = {k: np.asarray(v) for k, v in inp.items()}
    L0 = lambda k: g["L0_conv_" + k]
    parts = {}
    parts["mean"] = np.full((128, 128), 1.0 / C, np.float32)
    parts["ident"] = np.eye(128, dtype=np.float32)
    qkv = L0("qkv_w")
    for n, k in enumerate(("wq", "wk")):
        t = qkv[128 * n:128 * n + 128].T.reshape(C, HEADS, 1, HD)
        parts[k] = np.broadcast_to(t, (C, HEADS, 3, HD)).reshape(C, 384)
    parts["wv"] = qkv[256:384].T
    pw = L0("proj_w").T.reshape(HEADS, HD, C).transpose(1, 0, 2).reshape(1, HD, 512)
    parts["proj"] = np.concatenate([np.broadcast_to(pw, (3, HD, 512)).reshape(96, 512), np.zeros((32, 512), np.float32)])
    parts["spread"] = np.full((128, 128), 1.0 / 32, np.float32)
    parts["head_bias"] = np.stack([L0("proj_b")] + [np.zeros(C, np.float32)] * (HEADS - 1), 1)
    parts["w1"] = L0("fc1_w").T
    parts["w2"] = L0("fc2_w").T.reshape(2, 128, C).transpose(1, 0, 2).reshape(128, 256)
    vec = {k: L0(k) for k in ("ln1_w", "ln1_b", "ln2_w", "ln2_b", "fc2_b")}
    vec["fc1_b0"], vec["fc1_b1"] = L0("fc1_b")[:128], L0("fc1_b")[128:]
    vec["eps"] = np.full(128, EPS, np.float32)
    M = lambda k: g["L1_conv_" + k]
    parts["conv"] = M("conv_w").transpose(1, 2, 3, 0).reshape(C, 9 * C)
    in_w = M("in_proj_w")
    xi, taps, gate = (np.zeros((L, F, L, E), np.float32) for _ in range(3))
    for t in range(L):
        gate[t, :, t, :] = in_w[E:].T
        for k in range(DCONV):
            if t - (DCONV - 1) + k >= 0:
                xi[t - (DCONV - 1) + k, :, t, :] = in_w[:E].T
                taps[t - (DCONV - 1) + k, :, t, :] = M("conv1d_w")[:, 0, k]
    parts["xi"], parts["z"] = xi.reshape(128, 256), gate.reshape(128, 256)
    x_w = M("x_proj_w")
    dt_col, dt_row, bc, o_w = (np.zeros((4, E, 4, n), np.float32) for n in (E, E, 2 * ST_N, F))
    for t in range(4):
        dt_col[t, :, t, :] = x_w[0][:, None]
        dt_row[t, :, t, :] = M("dt_proj_w")[:, 0]
        bc[t, :, t, :] = x_w[1:].T
        o_w[t, :, t, :] = M("out_proj_w").T
    parts["dt"], parts["bc"], parts["out"] = dt_col.reshape(128, 128), bc.reshape(128, 128), o_w.reshape(128, 64)
    row = np.arange(128)
    parts["sum"] = (row % 32 == 8 * (row // 32) + row[:, None] // 16).astype(np.float32)
    n_group = C // GROUPS * N
    parts["group"] = np.where(row[:, None] // 32 == row // 32, np.float32(1.0 / n_group), np.float32(0))
    parts["A"] = M("A_log").reshape(GR, 128).T
    vec.update(conv_b=M("conv_b"), gn_w=M("gn_w"), gn_b=M("gn_b"), conv1d_b=np.tile(M("conv1d_b"), 4),
               dt_b=np.tile(M("dt_proj_b"), 4), D=np.tile(M("D"), 4))
    parts["vecs"] = np.stack([vec[k] for k in VECS], 1)
    wide = np.arange(512)
    of = row[:96, None] % 32
    pad = lambda a: np.concatenate([a.astype(np.float32), np.zeros((32, a.shape[1]), np.float32)])
    raws = {"conv1d": taps.reshape(128, 256), "dt_row": dt_row.reshape(128, 128),
            "spread_e": pad(of == wide // 16), "spread_b": pad(of == row % 16), "spread_c": pad(of == 16 + row % 16)}
    join = lambda d, keys: np.ascontiguousarray(np.concatenate([np.asarray(d[k], np.float32) for k in keys], 1))
    return join(parts, WIDTHS), join(raws, RAW)


def kernel(**inputs):
    import concourse.bacc as bacc
    from concourse.bass_utils import run_bass_kernel_spmd

    nc = bacc.Bacc("TRN2", target_bir_lowering=False, num_devices=1)
    x = np.ascontiguousarray(inputs["x"])
    consts, raws = layout(inputs)
    x_in = nc.dram_tensor("x_in", x.shape, F32, kind="ExternalInput").ap()
    c_in = nc.dram_tensor("consts_in", consts.shape, F32, kind="ExternalInput").ap()
    r_in = nc.dram_tensor("raw_in", raws.shape, F32, kind="ExternalInput").ap()
    out = nc.dram_tensor("out", x.shape, F32, kind="ExternalOutput").ap()
    build(nc, x_in, c_in, r_in, out, x.shape[0])
    r = run_bass_kernel_spmd(nc, [{"x_in": x, "consts_in": consts, "raw_in": raws}], core_ids=[0])
    return r.results[0]["out"]
```

```python
from contextlib import ExitStack

import numpy as np

import concourse.bass as bass
from concourse import mybir

F32 = mybir.dt.float32
F16 = mybir.dt.float16
BF16 = mybir.dt.bfloat16
ALU = mybir.AluOpType
ACT = mybir.ActivationFunctionType
AX = mybir.AxisListType

C = 128
HEADS, HD = 4, 32
SIDE = 64
PAD = SIDE + 2
N = SIDE * SIDE
TC = 512
NCH = N // TC
ROWS = TC // SIDE
NJ = HEADS * NCH
KB = N // 128
UNITS = KB // 2
LAG = 3
NB = 4
TILES = 4 * NCH
EPS = 1e-5
QS = 16.0
SCALE = 1.0 / (QS * QS * float(np.sqrt(HD)))
ROW = 256.0
SHIFT = 14 * float(np.log(2)) / (SCALE * ROW)
SUB = "PPDPPPDPPPDPPPDP"


def upto(table, key, u):
    return sum(t == key for t in table[:u + 1])


SUB_P, SUB_D = SUB.count("P"), SUB.count("D")

START = 1

L, F, E, ST_N, DCONV = 8, 16, 32, 16, 4
NQ = SIDE // 4
SEQ = 2 * C
COLS = L * SEQ
GR = E * ST_N // 128
KINDS = ("bc", "dt", "u")
PARTS = 3
GROUPS = 4
HC_DVE = set()
CHAIN = 14

VECS = ["ln1_w", "ln1_b", "ln2_w", "ln2_b", "fc1_b0", "fc1_b1", "fc2_b", "eps",
        "conv_b", "gn_w", "gn_b", "conv1d_b", "dt_b", "D"]
WIDTHS = {"mean": 128, "ident": 128, "wq": 384, "wk": 384, "wv": 128, "proj": 512, "spread": 128, "head_bias": 4,
          "w1": 256, "w2": 256, "vecs": len(VECS), "conv": 9 * 128, "xi": 256, "z": 256, "dt": 128, "bc": 128,
          "out": 64, "sum": 128, "group": 128, "A": GR}
RAW = {"conv1d": 256, "dt_row": 128, "spread_e": 512, "spread_b": 128, "spread_c": 128}


def build(nc, x_in, consts_in, raw_in, out, B):
    at, pos, raw_at, raw_pos = {}, 0, {}, 0
    for k, width in WIDTHS.items():
        at[k] = pos
        pos += width
    for k, width in RAW.items():
        raw_at[k] = raw_pos
        raw_pos += width
    with ExitStack() as ctx:
        sb = lambda name, shape, dt=F32: ctx.enter_context(nc.sbuf_tensor(name, shape, dt))
        sem = lambda name: ctx.enter_context(nc.semaphore(name))

        cst = sb("cst", [128, pos])
        x = sb("x", [128, N])
        x2 = sb("x2", [128, PAD, PAD])
        spread = sb("spread_bf", [128, 768], BF16)
        negA = sb("negA", [128, GR])
        ARENA = 149 * 256
        arena = sb("arena", [128, ARENA])
        used = [0]

        def take(shape, dt=F32):
            size = int(np.prod(shape)) // (1 if dt == F32 else 2)
            assert used[0] + size <= ARENA, (used[0] + size, ARENA)
            a = arena[:, used[0]:used[0] + size]
            used[0] += size
            if dt != F32:
                a = a.bitcast(dt)
            if len(shape) == 2:
                a = a.rearrange("p (a b) -> p a b", a=shape[0])
            elif len(shape) == 3:
                a = a.rearrange("p (a b c) -> p a b c", a=shape[0], b=shape[1])
            return a

        qst = take([HEADS * N], F16)
        kst = take([HEADS * N], F16)
        vst = take([HEADS * KB * 128], BF16)
        at_p = used[0]
        p32 = take([NB, 1024])
        p1 = p32.rearrange("p b n -> p (b n)").bitcast(BF16).rearrange("p (b n e) -> p b n e", b=NB, e=2)[:, :, :, 1]
        p2 = take([NB, 1024], F16)
        osb, lns, rcp = take([TC]), take([TC]), take([TC])
        onrm = take([TC])[0:96, :]
        mx, cneg = take([TILES]), take([4])
        crow = take([128])[0:4, :]
        chi, clo = take([128], F16)[0:4, :], take([128], F16)[0:4, :]
        pcur = take([128])[0:96, :]
        used[0] = at_p
        xc, sq, rstd, z, xln, hid = (take([2, TC]) for _ in range(6))
        lnv, vres = take([TC]), take([TC])
        at_final = used[0]
        used[0] = 0
        dA, dbx = take([2, COLS]), take([2, COLS])
        hs = take([2, COLS])
        hC = take([2, COLS])
        bsb, csb = take([COLS]), take([COLS])
        stk = take([2, len(KINDS) * COLS], BF16)
        pcs = take([PARTS, len(KINDS) * TC], BF16)
        bc1 = take([TC], BF16)
        yc, yT = take([SEQ]), take([SEQ])
        xcs, szs = take([4, TC]), take([4, TC])
        mdt, dts, us, rbc, rdt, ru, ya, ym = (take([TC]) for _ in range(8))
        edt = ldt = mdt
        gs, gsums = take([8]), take([NQ])
        used[0] = 0
        raw = take([raw_pos])
        used[0] = at_final
        fin = take([N])
        xr = x
        ps = ctx.enter_context(nc.psum_tensor("ps", [128, 8, TC], F32))

        w = lambda k: cst[:, at[k]:at[k] + WIDTHS[k]]
        vec = lambda k: cst[:, at["vecs"] + VECS.index(k):at["vecs"] + VECS.index(k) + 1]

        S = {n: sem("s_" + n) for n in (
            "cst x x0 init mean xc sq var ln rstd z xln xlnfree qk q1 q2 v v1 vr v2 v3 "
            "sm red cneg ct crow chi clo cdma st p32  subp subd pv oev lns rcp bc on pcur proj tbfree "
            "fc1 gelu fc2 x2 out seen fill "
            "raw prep dz conv yc tr yT xi zz xcs szs dtp bcp bc1 rbc m e l dt parts pcs stk "
            "bcu bcev dtu uu da dbx scan hcp hcd y ya ym outp xr gsum gmm gmu gsq gvv gln grs gsc gxp fin gsc2 step").split()}
        (s_cst, s_x, s_x0, s_init, s_mean, s_xc, s_sq, s_var, s_ln, s_rstd, s_z, s_xln, s_xlnfree, s_qk, s_q1, s_q2, s_v, s_v1,
         s_vr, s_v2, s_v3, s_sm, s_red, s_cneg, s_ct, s_crow, s_chi, s_clo, s_cdma, s_st, s_p32, 
         s_subp, s_subd, s_pv, s_oev, s_lns, s_rcp, s_bc, s_on, s_pcur, s_proj, s_tbfree, s_fc1, s_gelu,
         s_fc2, s_x2, s_out, s_seen, s_fill, s_raw, s_prep, s_dz, s_conv, s_yc, s_tr, s_yT, s_xi, s_zz, s_xcs, s_szs,
         s_dtp, s_bcp, s_bc1, s_rbc, s_m, s_e, s_l, s_dt, s_parts, s_pcs, s_stk, s_bcu, s_bcev, s_dtu,
         s_uu, s_da, s_dbx, s_scan, s_hcp, s_hcd, s_y, s_ya, s_ym, s_outp, s_xr, s_gsum, s_gmm, s_gmu, s_gsq,
         s_gvv, s_gln, s_grs, s_gsc, s_gxp, s_fin, s_gsc2, s_step) = S.values()

        MEAN, VAR, QK, VB = 0, 1, 2, 6
        ST, SM, OB, TB = 0, 4, 6, 7
        FC1, FC2 = 2, 4
        DT, UU, CB, YB, SA, SB = 0, 2, 4, 5, 6, 7

        block = ctx.enter_context(nc.Block())
        ds = bass.ds

        def slot(t, f):
            return t.rearrange("p a b -> p (a b)")[:, ds((f & 3) * TC, TC)]

        def part_of(what, f, part):
            return pcs[:, part, TC * KINDS.index(what):TC * KINDS.index(what) + TC]

        def stack(what, q, n):
            at = KINDS.index(what) * COLS + n * TC
            return stk.rearrange("p a n -> p (a n)")[0:96, ds((q & 1) * (len(KINDS) * COLS) + at, TC)]

        def times_c(eng, api, Q, g, first, done):
            
            eng.wait_ge(s_scan, Q * GR + g + 1)
            if g == min(set(range(GR)) - HC_DVE) or g in HC_DVE:
                eng.wait_ge(s_bcev, Q * 8 + 8)
            if not (first and g < 2):
                eng.wait_ge(s_y, Q * GR + g - 1)
            api.tensor_tensor(hC[:, g % 2, :].rearrange("p (t n) -> p t n", t=L),
                              hs[:, g % 2, :].rearrange("p (n t) -> p t n", t=L),
                              csb[:, :].rearrange("p (t n) -> p t n", t=L), ALU.mult).then_inc(done, 1)

        def v_psum():
            return ps[:, VB, :].rearrange("p (k h d) -> p k h d", k=4, h=HEADS)

        def v_part(part, i):
            v = vst[:, :].rearrange("p (h k m) -> p k h m", h=HEADS, k=KB)
            return v[:, ds(i * 4, 4), :, HD * part:HD * part + HD]

        def vres4():
            return vres[:, :].rearrange("p (k h d) -> p k h d", k=4, h=HEADS)

        def head_base(j):
            return (j & (NJ - NCH)) * TC

        def chunks(eng, body):
            with eng.Fori(0, NCH // 2 - 1) as t:
                body(2 * t, 0, True)
                body(2 * t + 1, 1, True)
            body(NCH - 2, 0, True)
            body(NCH - 1, 1, False)

        def mchunks(eng, body):
            body(0, True, True, True, False)
            body(1, False, True, True, False)
            with eng.Fori(0, NQ - 4) as t:
                body(t + 2, False, True, True, True)
            body(NQ - 2, False, False, True, True)
            body(NQ - 1, False, False, False, True)

        HCD, HCP = len(HC_DVE), GR - len(HC_DVE)

        def wait_hc(eng, Q, g):
            if g in HC_DVE:
                eng.wait_ge(s_hcd, Q * HCD + sum(i in HC_DVE for i in range(g + 1)))
            else:
                eng.wait_ge(s_hcp, Q * HCP + sum(i not in HC_DVE for i in range(g + 1)))

        def tn(t, k):
            return t.rearrange("p (n t) -> p t n", t=L)[:, 2 * k:2 * k + 2, :]

        def nt(t, k):
            return t.rearrange("p (h t n) -> p t h n", h=2, t=4)[:, k, :, :]

        def qchunks(eng, body):
            body(0, True, True, True)
            with eng.Fori(0, NJ - 3) as t:
                body(t + 1, False, True, True)
            body(NJ - 2, False, True, False)
            body(NJ - 1, False, False, False)

        @block.tensor
        def _(pe):
            def mean(i, L):
                pe.wait_ge(s_xc, START + L)
                nc.tensor.matmul(ps[:, MEAN, :], w("mean"), x[:, ds(i * TC, TC)],
                                 start=True, stop=True).then_inc(s_mean, 1)

            def var(par, L):
                pe.wait_ge(s_sq, L + 1)
                pe.wait_ge(s_ln, START + L)
                nc.tensor.matmul(ps[:, VAR, :], w("mean"), sq[:, par, :],
                                 start=True, stop=True).then_inc(s_var, 1)

            def project(par, K, which):
                for h in range(HEADS):
                    k = h + (HEADS if which == "wk" else 0)
                    pe.wait_ge(s_q2, K + k + 1)
                    nc.tensor.matmul(ps[0:96, QK + h, :], w(which)[:, 96 * h:96 * h + 96], xln[:, par, :],
                                     start=True, stop=True).then_inc(s_qk, 1)

            pe.wait_ge(s_cst, 16)
            pe.wait_ge(s_prep, 6)
            pe.sem_inc(s_pv, NB)
            for q in (s_proj, s_fc2, s_outp):
                pe.sem_inc(q, START)
            with pe.Fori(0, B) as b:
                pe.wait_ge(s_x0, (b + 1) * 16)
                L0 = b * 2 * NCH
                mean(0, L0)
                var(0, L0)

                def qkv(i, par, more):
                    K = (b * NCH + i) * 2 * HEADS
                    if more:
                        pe.wait_ge(s_x, (b + 1) * 48)
                        mean(i + 1, L0 + i + 1)
                    pe.wait_ge(s_xln, L0 + i + 1)
                    project(par, K, "wq")
                    if more:
                        var(1 - par, L0 + i + 1)
                    project(par, K, "wk")
                    pe.wait_ge(s_vr, START + b * NCH + i)
                    for t in range(4):
                        mm = nc.tensor.matmul(ps[:, VB, 128 * t:128 * t + 128], xln[:, par, 128 * t:128 * t + 128],
                                              w("wv"), start=True, stop=True)
                    mm.then_inc(s_v, 1)
                chunks(pe, qkv)

                def max_tile(j, m, head):
                    pe.wait_ge(s_red, (b * NJ + j) * TILES + m + 1)
                    nc.tensor.matmul(ps[:, SM + m % 2, :], qst[0:96, ds(j * TC + m // NCH * 128, 128)],
                                     kst[0:96, ds(head + m % NCH * TC, TC)],
                                     start=True, stop=True).then_inc(s_sm, 1)

                def scores(j, u, head):
                    if not (isinstance(j, int) and j == 0 and u < 2):
                        pe.wait_ge(s_p32, (b * NJ + j) * UNITS + u - 1)
                    if u == 0:
                        pe.wait_ge(s_cdma, 32 * (b * NJ + j + 1))
                    for t in range(2):
                        mm = nc.tensor.matmul(ps[:, ST + 2 * (u % 2) + t, :],
                                              kst[0:98, ds(head + (2 * u + t) * 128, 128)],
                                              qst[0:98, ds(j * TC, TC)], start=True, stop=True)
                    mm.then_inc(s_st, 1)

                def pv(j, u, head):
                    J = b * NJ + j
                    if SUB[u] == "P":
                        pe.wait_ge(s_subp, J * SUB_P + upto(SUB, "P", u))
                    else:
                        pe.wait_ge(s_subd, J * SUB_D + upto(SUB, "D", u))
                    if u == 0:
                        pe.wait_ge(s_oev, START + J)
                    for t in range(2):
                        for n, part in enumerate((p1, p2)):
                            mm = nc.tensor.matmul(ps[:, OB, :], vst[:, ds(head + (2 * u + t) * 128, 128)],
                                                  part[:, u % NB, TC * t:TC * t + TC],
                                                  start=(u == 0 and t == 0 and n == 0),
                                                  stop=(u == UNITS - 1 and t == 1 and n == 1))
                    mm.then_inc(s_pv, 1)

                def turn_max(idx, J):
                    pe.wait_ge(s_cneg, J + 1)
                    pe.wait_ge(s_tbfree, b * 3 * NJ + idx + 1)
                    nc.tensor.transpose(ps[0:4, TB, 0:128], cneg[:, :], w("ident")).then_inc(s_ct, 1)

                def spread_sums(idx, J):
                    pe.wait_ge(s_rcp, J + 1)
                    pe.wait_ge(s_tbfree, b * 3 * NJ + idx + 1)
                    nc.tensor.matmul(ps[0:96, TB, :], w("spread")[96:128, 0:96], rcp[96:128, :],
                                     start=True, stop=True).then_inc(s_bc, 1)

                def out_project(idx, J):
                    pe.wait_ge(s_on, START + J + 1)
                    pe.wait_ge(s_pcur, J + 1)
                    pe.wait_ge(s_tbfree, b * 3 * NJ + idx + 1)
                    nc.tensor.matmul(ps[:, TB, :], pcur[:, :], onrm[:, :],
                                     start=True, stop=True).then_inc(s_proj, 1)

                pe.wait_ge(s_fill, 2 * b + 2)
                pe.wait_ge(s_q2, 4 + (b + 1) * NCH * 2 * HEADS)
                for m in range(TILES):
                    max_tile(0, m, 0)
                turn_max(0, b * NJ)
                for m in range(TILES):
                    max_tile(1, m, 0)
                pe.wait_ge(s_v3, START + (b + 1) * NCH)
                for u in range(LAG):
                    scores(0, u, 0)

                def attend(j, first, has_next, has_max):
                    J = b * NJ + j
                    base = 2 + 3 * (j - 1) if not first else 1
                    for u in range(UNITS):
                        if u + LAG < UNITS:
                            scores(j, u + LAG, head_base(j))
                        elif has_next:
                            scores(j + 1, u + LAG - UNITS, head_base(j + 1))
                        if has_max:
                            for m in (2 * u, 2 * u + 1):
                                max_tile(j + 2, m, head_base(j + 2))
                        pv(j, u, head_base(j))
                        if u == 1 and has_next:
                            turn_max(base, J + 1)
                        if u == 4 and not first:
                            spread_sums(base + has_next, J - 1)
                        if u == 8 and not first:
                            out_project(base + has_next + 1, J - 1)
                qchunks(pe, attend)
                spread_sums(3 * NJ - 2, b * NJ + NJ - 1)
                out_project(3 * NJ - 1, b * NJ + NJ - 1)

                pe.wait_ge(s_tbfree, 1 + (b + 1) * 3 * NJ)
                mean(0, L0 + NCH)
                var(0, L0 + NCH)

                def mlp(i, par, more):
                    L = L0 + NCH + i
                    G = b * NCH + i
                    if more:
                        mean(i + 1, L + 1)
                    pe.wait_ge(s_xln, L + 1)
                    pe.wait_ge(s_gelu, START + 2 * G)
                    for n in range(2):
                        nc.tensor.matmul(ps[:, FC1 + n, :], w("w1")[:, 128 * n:128 * n + 128], xln[:, par, :],
                                         start=True, stop=True).then_inc(s_fc1, 1)
                    if more:
                        var(1 - par, L + 1)
                    pe.wait_ge(s_gelu, START + 2 * G + 2)
                    pe.wait_ge(s_x2, START + G)
                    for n in range(2):
                        mm = nc.tensor.matmul(ps[:, FC2, :], w("w2")[:, 128 * n:128 * n + 128], hid[:, n, :],
                                              start=(n == 0), stop=(n == 1))
                    mm.then_inc(s_fc2, 1)
                chunks(pe, mlp)

                Q0 = b * NQ

                def conv(f, half):
                    if half == 0:
                        if not isinstance(f, int):
                            pe.wait_ge(s_xr, START + Q0 + f - 3)
                        if not (isinstance(f, int) and f == 0):
                            pe.wait_ge(s_dt, Q0 + f)
                    for n in range(5) if half == 0 else range(5, 9):
                        rows = x2[:, ds(4 * f + n // 3, 4), n % 3:n % 3 + SIDE]
                        mm = nc.tensor.matmul(ps[:, SA, 0:SEQ].rearrange("p (r w) -> p r w", r=4),
                                              w("conv")[:, 128 * n:128 * n + 128], rows,
                                              start=(n == 0), stop=(n == 8))
                    if half == 1:
                        mm.then_inc(s_conv, 1)

                def turn(f):
                    pe.wait_ge(s_yc, Q0 + f + 1)
                    if not (isinstance(f, int) and f == 0):
                        pe.wait_ge(s_rbc, Q0 + f)
                    for r in range(2):
                        mm = nc.tensor.transpose(ps[:, SB, C * r:C * r + C], yc[:, C * r:C * r + C], w("ident"))
                    mm.then_inc(s_tr, 1)

                def in_project(f):
                    pe.wait_ge(s_yT, Q0 + f + 1)
                    for k, bank, s_k in (("xi", SA, s_xi), ("z", SB, s_zz)):
                        for n in range(2):
                            mm = nc.tensor.matmul(ps[:, bank, SEQ * n:SEQ * n + SEQ],
                                                  w(k)[:, 128 * n:128 * n + 128], yT[:, :], start=True, stop=True)
                        mm.then_inc(s_k, 1)

                def x_project(f):
                    pe.wait_ge(s_xcs, Q0 + f + 1)
                    pe.wait_ge(s_szs, Q0 + f + 1)
                    nc.tensor.matmul(ps[:, SA, :], w("dt"), slot(xcs, f), start=True, stop=True).then_inc(s_dtp, 1)
                    nc.tensor.matmul(ps[:, SB, :], w("bc"), slot(xcs, f), start=True, stop=True).then_inc(s_bcp, 1)

                def spread_bc(q, n):
                    sel = spread[0:96, 512 + 128 * (n // 4):640 + 128 * (n // 4)]
                    nc.tensor.matmul(ps[:, n if n < 4 else CB, :], sel, stack("bc", q, n % 4),
                                     start=True, stop=True).then_inc(s_bcu, 1)

                def spread_b(q, first):
                    Q = Q0 + q
                    pe.wait_ge(s_stk, 16 * 12 * (Q + 1))
                    for n in range(4):
                        if n == 0 and not first:
                            pe.wait_ge(s_da, Q * 16)
                        if n == 2 and not first:
                            pe.wait_ge(s_dbx, Q * 16)
                        spread_bc(q, n)

                def spread_c(q, n):
                    pe.wait_ge(s_bcev, (Q0 + q) * 8 + n)
                    spread_bc(q, n)

                def spread_group(q, g, which):
                    Q = Q0 + q
                    sel = spread[0:96, 128 * g:128 * g + 128]
                    for k in which:
                        n = Q * 16 + g * 4 + k
                        if g == 0 and k < 2:
                            pe.wait_ge(s_bcev, Q * 8 + 1 + k)
                        else:
                            pe.wait_ge(s_da, n - 1)
                        nc.tensor.matmul(ps[:, DT + k % 2, :], sel, stack("dt", q, k),
                                         start=True, stop=True).then_inc(s_dtu, 1)
                        if g == 0 and k < 2:
                            pe.wait_ge(s_bcev, Q * 8 + 3 + k)
                        else:
                            pe.wait_ge(s_dbx, n - 1)
                        nc.tensor.matmul(ps[:, UU + k % 2, :], sel, stack("u", q, k),
                                         start=True, stop=True).then_inc(s_uu, 1)

                def sum_states(q, g, first):
                    Q = Q0 + q
                    wait_hc(pe, Q, g)
                    if g == 0 and not first:
                        pe.wait_ge(s_ya, Q)
                    for t in range(4):
                        mm = nc.tensor.matmul(ps[32 * t:32 * t + 32, YB, :], w("sum")[:, 32 * g:32 * g + 32],
                                              nt(hC[:, g % 2, :], t), start=(g == 0), stop=(g == GR - 1))
                    mm.then_inc(s_y, 1)

                def out_project(q, fronts):
                    pe.wait_ge(s_ym, START + Q0 + q + 1)
                    pe.wait_ge(s_dt, Q0 + fronts)
                    pe.wait_ge(s_xr, START + Q0 + q)
                    for r in range(2):
                        for n in range(2):
                            mm = nc.tensor.matmul(ps[:, SA, 128 * r + 64 * n:128 * r + 64 * n + 64],
                                                  ym[:, SEQ * n + C * r:SEQ * n + C * r + C], w("out"),
                                                  start=True, stop=True)
                    mm.then_inc(s_outp, 1)

                pe.wait_ge(s_x2, START + (b + 1) * NCH)
                for f in range(2):
                    conv(f, 0)
                    conv(f, 1)
                    turn(f)
                    in_project(f)
                    x_project(f)

                def scan_chunk(q, first, has_front, has_next, has_out):
                    fronts = q + 2 if has_front else NQ
                    spread_b(q, first)
                    spread_group(q, 0, (0,))
                    spread_group(q, 0, (1,))
                    if not first:
                        sum_states(q - 1, 2, False)
                    spread_group(q, 0, (2,))
                    spread_group(q, 0, (3,))
                    spread_c(q, 4)
                    spread_c(q, 5)
                    spread_group(q, 1, (0,))
                    spread_c(q, 6)
                    spread_group(q, 1, (1,))
                    spread_c(q, 7)
                    if has_out:
                        out_project(q - 2, fronts)
                    if has_front:
                        conv(q + 2, 0)
                    spread_group(q, 1, (2,))
                    spread_group(q, 1, (3,))
                    if not first:
                        sum_states(q - 1, 3, False)
                    if has_front:
                        conv(q + 2, 1)
                    spread_group(q, 2, (0,))
                    spread_group(q, 2, (1,))
                    if has_front:
                        turn(q + 2)
                    if has_front:
                        in_project(q + 2)
                    spread_group(q, 2, (2,))
                    spread_group(q, 2, (3,))
                    sum_states(q, 0, first)
                    spread_group(q, 3, (0,))
                    spread_group(q, 3, (1,))
                    if has_front:
                        x_project(q + 2)
                    spread_group(q, 3, (2,))
                    spread_group(q, 3, (3,))
                    sum_states(q, 1, first)
                mchunks(pe, scan_chunk)
                out_project(NQ - 2, NQ)
                sum_states(NQ - 1, 2, False)
                sum_states(NQ - 1, 3, False)
                out_project(NQ - 1, NQ)

                pe.wait_ge(s_xr, START + (b + 1) * NQ)
                nc.tensor.matmul(ps[:, SB, 0:NQ], w("group"), gsums[:, :], start=True, stop=True).then_inc(s_gmm, 1)
                pe.wait_ge(s_gsq, b + 1)
                nc.tensor.matmul(ps[:, SB, 0:1], w("group"), gs[:, 2:3], start=True, stop=True).then_inc(s_gvv, 1)

        @block.scalar
        def _(act):
            def square(par, L):
                act.wait_ge(s_xc, START + L + 1)
                nc.scalar.activation(sq[:, par, :], xc[:, par, :], ACT.Square).then_inc(s_sq, 1)

            def inverse_deviation(par, L):
                act.wait_ge(s_var, L + 1)
                nc.scalar.activation(lnv[:, :], ps[:, VAR, :], ACT.Ln, bias=vec("eps")).then_inc(s_ln, 1)
                act.wait_ge(s_ln, START + L + 1)
                nc.scalar.activation(rstd[:, par, :], lnv[:, :], ACT.Exp, scale=-0.5).then_inc(s_rstd, 1)

            act.wait_ge(s_cst, 16)
            for q in (s_ln, s_oev, s_gelu, s_xr):
                act.sem_inc(q, START)
            act.wait_ge(s_raw, 16)
            nc.scalar.activation(spread[:, :], raw[:, raw_at["spread_e"]:raw_at["spread_e"] + 768],
                                 ACT.Copy).then_inc(s_prep, 1)
            nc.scalar.activation(negA[:, :], w("A"), ACT.Exp).then_inc(s_prep, 1)
            act.wait_ge(s_prep, 6)
            with act.Fori(0, B) as b:
                L0 = b * 2 * NCH
                nc.scalar.preload_act_table_set("natural_log_exp_and_others")
                square(0, L0)
                inverse_deviation(0, L0)

                def qkv(i, par, more):
                    L = L0 + i
                    K = (b * NCH + i) * 2 * HEADS
                    if more:
                        square(1 - par, L + 1)
                    for k in range(2 * HEADS):
                        if k == HEADS and more:
                            inverse_deviation(1 - par, L + 1)
                        act.wait_ge(s_qk, K + k + 1)
                        st = qst if k < HEADS else kst
                        h = k % HEADS
                        nc.scalar.activation(st[0:96, ds(i * TC + h * N, TC)], ps[0:96, QK + h, :],
                                             ACT.Copy, scale=QS).then_inc(s_q1, 1)
                    act.wait_ge(s_v, b * NCH + i + 1)
                    nc.scalar.activation(v_part(0, i), v_psum(), ACT.Copy).then_inc(s_v1, 1)
                chunks(act, qkv)

                def attend(j, first, has_next, has_max):
                    J = b * NJ + j
                    for u in range(UNITS):
                        n = J * UNITS + u
                        act.wait_ge(s_st, n + 1)
                        act.wait_ge(s_pv, n + 1)
                        src = ps[:, ST + 2 * (u % 2):ST + 2 * (u % 2) + 2, :]
                        nc.scalar.activation(p32[:, u % NB, :], src, ACT.Exp, scale=SCALE).then_inc(s_p32, 1)
                        if u == 1 and not first:
                            read_sums(J - 1)

                def read_sums(J):
                    act.wait_ge(s_pv, NB + (J + 1) * UNITS)
                    act.wait_ge(s_on, START + J)
                    nc.scalar.activation(osb[:, :], ps[:, OB, :], ACT.Copy).then_inc(s_oev, 1)
                    act.wait_ge(s_oev, START + J + 1)
                    nc.scalar.activation(lns[96:128, :], osb[96:128, :], ACT.Ln).then_inc(s_lns, 1)
                    act.wait_ge(s_lns, J + 1)
                    nc.scalar.activation(rcp[96:128, :], lns[96:128, :], ACT.Exp, scale=-1.0).then_inc(s_rcp, 1)
                nc.scalar.preload_act_table_set("natural_log_exp_and_others")
                qchunks(act, attend)
                read_sums(b * NJ + NJ - 1)

                square(0, L0 + NCH)
                inverse_deviation(0, L0 + NCH)

                def mlp(i, par, more):
                    L = L0 + NCH + i
                    G = b * NCH + i
                    if more:
                        square(1 - par, L + 1)
                    for n in range(2):
                        act.wait_ge(s_fc1, 2 * G + n + 1)
                        if n == 0:
                            act.wait_ge(s_fc2, START + G)
                        nc.scalar.activation(hid[:, n, :], ps[:, FC1 + n, :], ACT.Gelu,
                                             bias=vec(f"fc1_b{n}")).then_inc(s_gelu, 1)
                    nc.scalar.preload_act_table_set("natural_log_exp_and_others")
                    if more:
                        inverse_deviation(1 - par, L + 1)
                chunks(act, mlp)

                Q0 = b * NQ

                def front_a(f):
                    act.wait_ge(s_conv, Q0 + f + 1)
                    nc.scalar.activation(yc[:, :], ps[:, SA, 0:SEQ], ACT.Identity, bias=vec("conv_b")).then_inc(s_yc, 1)

                def front_b(f):
                    act.wait_ge(s_tr, Q0 + f + 1)
                    nc.scalar.activation(yT[:, :], ps[:, SB, 0:SEQ], ACT.Copy).then_inc(s_yT, 1)

                def front_silu(f):
                    act.wait_ge(s_xi, Q0 + f + 1)
                    if not isinstance(f, int):
                        act.wait_ge(s_ym, START + Q0 + f - 3)
                    nc.scalar.activation(slot(xcs, f), ps[:, SA, :], ACT.Silu, bias=vec("conv1d_b")).then_inc(s_xcs, 1)
                    act.wait_ge(s_zz, Q0 + f + 1)
                    nc.scalar.activation(slot(szs, f), ps[:, SB, :], ACT.Silu).then_inc(s_szs, 1)
                    nc.scalar.preload_act_table_set("natural_log_exp_and_others")

                def front_c(f):
                    act.wait_ge(s_bcp, Q0 + f + 1)
                    if not (isinstance(f, int) and f == 0):
                        act.wait_ge(s_parts, (Q0 + f) * 4 - 2)
                    nc.scalar.activation(bc1[:, :], ps[:, SB, :], ACT.Copy).then_inc(s_bc1, 1)

                def front_s(f):
                    act.wait_ge(s_m, Q0 + f + 1)
                    nc.scalar.activation(edt[:, :], mdt[:, :], ACT.Exp).then_inc(s_e, 1)
                    act.wait_ge(s_e, Q0 + f + 1)
                    nc.scalar.activation(ldt[:, :], edt[:, :], ACT.Ln, bias=1.0).then_inc(s_l, 1)

                def copy_bc(q, first, which):
                    Q = Q0 + q
                    for n in which:
                        if n == 0 and not first:
                            act.wait_ge(s_dbx, Q * 16)
                        if n == 4 and not first:
                            wait_hc(act, Q - 1, GR - 1)
                            wait_hc(act, Q - 1, GR - 2)
                        act.wait_ge(s_bcu, Q * 8 + n + 1)
                        bank = n if n < 4 else CB
                        dst = (bsb if n < 4 else csb)[:, TC * (n % 4):TC * (n % 4) + TC]
                        nc.scalar.activation(dst, ps[:, bank, :], ACT.Copy).then_inc(s_bcev, 1)

                def decays(q, g, which, first):
                    Q = Q0 + q
                    if 0 in which and not (first and g < 2):
                        act.wait_ge(s_scan, Q * GR + g - 1)
                    for k in which:
                        act.wait_ge(s_dtu, Q * 16 + g * 4 + k + 1)
                        lo = 1 if k == 0 else 0
                        src = ps[:, DT + k % 2, :].rearrange("p (t n) -> p t n", t=2)[:, lo:2, :]
                        nc.scalar.activation(tn(dA[:, g % 2, :], k)[:, lo:2, :], src, ACT.Exp,
                                             scale=negA[:, g:g + 1]).then_inc(s_da, 1)

                def out_rows(q):
                    act.wait_ge(s_outp, START + Q0 + q + 1)
                    nc.scalar.activation(xr[:, ds(q * SEQ, SEQ)], ps[:, SA, 0:SEQ], ACT.Copy,
                                         accum_out=gsums[:, ds(q, 1)]).then_inc(s_xr, 1)

                for f in range(2):
                    front_a(f)
                    front_b(f)
                    front_silu(f)
                    front_c(f)
                    front_s(f)

                def scan_chunk(q, first, has_front, has_next, has_out):
                    copy_bc(q, first, range(4))
                    decays(q, 0, (0,), first)
                    decays(q, 0, (1,), first)
                    decays(q, 0, (2,), first)
                    decays(q, 0, (3,), first)
                    copy_bc(q, first, (4,))
                    copy_bc(q, first, (5,))
                    decays(q, 1, (0,), first)
                    copy_bc(q, first, (6,))
                    decays(q, 1, (1,), first)
                    copy_bc(q, first, (7,))
                    if has_out:
                        out_rows(q - 2)
                    decays(q, 1, (2,), first)
                    decays(q, 1, (3,), first)
                    if has_front:
                        front_a(q + 2)
                    decays(q, 2, (0,), first)
                    decays(q, 2, (1,), first)
                    if has_front:
                        front_b(q + 2)
                    decays(q, 2, (2,), first)
                    decays(q, 2, (3,), first)
                    if has_front:
                        front_silu(q + 2)
                    decays(q, 3, (0,), first)
                    decays(q, 3, (1,), first)
                    decays(q, 3, (2,), first)
                    decays(q, 3, (3,), first)
                    if has_front:
                        front_c(q + 2)
                        front_s(q + 2)
                mchunks(act, scan_chunk)
                out_rows(NQ - 2)
                out_rows(NQ - 1)

                nc.scalar.preload_act_table_set("natural_log_exp_and_others")
                act.wait_ge(s_xr, START + Q0 + NQ)
                act.wait_ge(s_gmu, b + 1)
                nc.scalar.activation(fin[:, :], xr[:, :], ACT.Square, bias=gs[:, 1:2],
                                     accum_out=gs[:, 2:3]).then_inc(s_gsq, 1)
                act.wait_ge(s_gvv, b + 1)
                nc.scalar.activation(gs[:, 3:4], ps[:, SB, 0:1], ACT.Ln, bias=vec("eps")).then_inc(s_gln, 1)
                act.wait_ge(s_gln, b + 1)
                nc.scalar.activation(gs[:, 4:5], gs[:, 3:4], ACT.Exp, scale=-0.5).then_inc(s_grs, 1)
                act.wait_ge(s_gsc, b + 1)
                for n in range(4):
                    nc.scalar.activation(fin[:, 1024 * n:1024 * n + 1024], xr[:, 1024 * n:1024 * n + 1024], ACT.Silu,
                                         scale=gs[:, 5:6], bias=gs[:, 6:7]).then_inc(s_gxp, 1)

        @block.vector
        def _(dve):
            def centre(i, par, L):
                dve.wait_ge(s_mean, L + 1)
                nc.vector.tensor_tensor(xc[:, par, :], x[:, ds(i * TC, TC)], ps[:, MEAN, :],
                                        ALU.subtract).then_inc(s_xc, 1)

            def normalise(par, L):
                dve.wait_ge(s_rstd, L + 1)
                nc.vector.tensor_tensor(z[:, par, :], xc[:, par, :], rstd[:, par, :], ALU.mult).then_inc(s_z, 1)

            dve.sem_inc(s_q2, 4)
            dve.sem_inc(s_red, 2)
            dve.sem_inc(s_tbfree, 1)
            for q in (s_xc, s_vr, s_on, s_x2, s_ym):
                dve.sem_inc(q, START)
            dve.wait_ge(s_cst, 16)
            dve.wait_ge(s_raw, 16)
            r = lambda k: raw[:, raw_at[k]:raw_at[k] + RAW[k]]
            nc.vector.memset(x2[:, :, :], 0.0).then_inc(s_prep, 1)
            nc.vector.tensor_tensor(w("xi"), w("xi"), r("conv1d"), ALU.mult).then_inc(s_prep, 1)
            nc.vector.tensor_tensor(w("dt"), w("dt"), r("dt_row"), ALU.mult).then_inc(s_prep, 1)
            dve.wait_ge(s_prep, 5)
            nc.vector.tensor_scalar(negA[:, :], negA[:, :], -1.0, None, ALU.mult).then_inc(s_prep, 1)
            dve.wait_ge(s_prep, 6)
            with dve.Fori(0, B) as b:
                L0 = b * 2 * NCH
                centre(0, 0, L0)
                normalise(0, L0)

                def qkv(i, par, more):
                    L = L0 + i
                    K = (b * NCH + i) * 2 * HEADS
                    if more:
                        centre(i + 1, 1 - par, L + 1)
                    for k in range(2 * HEADS):
                        if k == HEADS and more:
                            normalise(1 - par, L + 1)
                        dve.wait_ge(s_q1, K + k + 1)
                        st, r = (qst, 64) if k < HEADS else (kst, 32)
                        h = k % HEADS
                        low = st[r:r + 32, ds(i * TC + h * N, TC)]
                        nc.vector.scalar_tensor_tensor(out=low, in0=ps[r:r + 32, QK + h, :], scalar=QS, in1=low,
                                                       op0=ALU.mult, op1=ALU.subtract).then_inc(s_q2, 1)
                    dve.wait_ge(s_v1, b * NCH + i + 1)
                    dve.wait_ge(s_v3, START + b * NCH + i)
                    nc.vector.tensor_tensor(vres4(), v_psum(), v_part(0, i), ALU.subtract).then_inc(s_vr, 1)
                chunks(dve, qkv)

                def reduce_tile(j, m):
                    T = (b * NJ + j) * TILES + m
                    dve.wait_ge(s_sm, T + 1)
                    nc.vector.tensor_reduce(mx[:, m:m + 1], ps[:, SM + m % 2, :], AX.X,
                                            ALU.max).then_inc(s_red, 1)

                def chunk_max(J):
                    dve.wait_ge(s_red, 2 + (J + 1) * TILES)
                    nc.vector.tensor_reduce(cneg[:, :], mx[:, :].rearrange("p (q t) -> p q t", q=4), AX.X,
                                            ALU.max, negate=True).then_inc(s_cneg, 1)

                def max_rows(J, first=False):
                    dve.wait_ge(s_ct, J + 1)
                    nc.vector.tensor_scalar(crow[:, :], ps[0:4, TB, 0:128], 1.0 / ROW, SHIFT,
                                            ALU.mult, ALU.add).then_inc(s_tbfree, 1)
                    if not first:
                        dve.wait_ge(s_cdma, 32 * J)
                    dve.wait_ge(s_tbfree, tb[0] + 1)
                    tb[0] = tb[0] + 1
                    nc.vector.tensor_copy(chi[:, :], crow[:, :]).then_inc(s_chi, 1)
                    dve.wait_ge(s_chi, J + 1)
                    nc.vector.tensor_tensor(clo[:, :], crow[:, :], chi[:, :], ALU.subtract).then_inc(s_clo, 1)

                def parts(j, u):
                    n = (b * NJ + j) * UNITS + u
                    if SUB[u] == "D":
                        dve.wait_ge(s_p32, n + 1)
                        nc.vector.tensor_tensor(p2[:, u % NB, :], p32[:, u % NB, :], p1[:, u % NB, :],
                                                ALU.subtract).then_inc(s_subd, 1)

                def scale_sums(J):
                    dve.wait_ge(s_bc, J + 1)
                    nc.vector.tensor_tensor(onrm[:, :], osb[0:96, :], ps[0:96, TB, :],
                                            ALU.mult).then_inc(s_on, 1)
                    dve.wait_ge(s_on, START + J + 1)
                    dve.sem_inc(s_tbfree, 1)

                def add_heads(j, J):
                    dve.wait_ge(s_proj, START + J + 1)
                    xs = x[:, ds((j & (NCH - 1)) * TC, TC)]
                    nc.vector.scalar_tensor_tensor(out=xs, in0=ps[:, TB, :], scalar=w("head_bias")[:, ds(j // NCH, 1)], in1=xs,
                                                   op0=ALU.add, op1=ALU.add).then_inc(s_tbfree, 1)

                tb = [None]
                dve.wait_ge(s_out, START + b * 64)
                for m in range(TILES):
                    reduce_tile(0, m)
                chunk_max(b * NJ)
                tb[0] = 1 + b * 3 * NJ
                max_rows(b * NJ, True)
                dve.wait_ge(s_cneg, b * NJ + 1)
                for m in range(TILES):
                    reduce_tile(1, m)
                parts(0, 0)

                def attend(j, first, has_next, has_max):
                    J = b * NJ + j
                    tb[0] = 1 + b * 3 * NJ + (1 if first else 2 + 3 * (j - 1))
                    if has_next:
                        chunk_max(J + 1)
                        dve.wait_ge(s_cneg, J + 2)
                    for u in range(UNITS):
                        if u + 1 < UNITS:
                            parts(j, u + 1)
                        elif has_next:
                            parts(j + 1, 0)
                        if has_max:
                            reduce_tile(j + 2, 2 * u)
                            reduce_tile(j + 2, 2 * u + 1)
                        if u == 2 and has_next:
                            max_rows(J + 1)
                        if u == 5 and not first:
                            scale_sums(J - 1)
                        if u == 9 and not first:
                            add_heads(j - 1, J - 1)
                qchunks(dve, attend)
                scale_sums(b * NJ + NJ - 1)
                add_heads(NJ - 1, b * NJ + NJ - 1)

                centre(0, 0, L0 + NCH)
                normalise(0, L0 + NCH)

                def mlp(i, par, more):
                    L = L0 + NCH + i
                    G = b * NCH + i
                    if more:
                        centre(i + 1, 1 - par, L + 1)
                        normalise(1 - par, L + 1)
                    dve.wait_ge(s_fc2, START + G + 1)
                    nc.vector.scalar_tensor_tensor(
                        out=x2[:, ds(i * ROWS + 1, ROWS), 1:SIDE + 1],
                        in0=ps[:, FC2, :].rearrange("p (r w) -> p r w", r=ROWS), scalar=vec("fc2_b"),
                        in1=x[:, ds(i * TC, TC)].rearrange("p (r w) -> p r w", r=ROWS),
                        op0=ALU.add, op1=ALU.add).then_inc(s_x2, 1)
                chunks(dve, mlp)

                Q0 = b * NQ

                def front_d(f):
                    FQ = Q0 + f
                    dve.wait_ge(s_dtp, FQ + 1)
                    nc.vector.tensor_scalar(mdt[:, :], ps[:, SA, :], vec("dt_b"), 30.0, ALU.add,
                                            ALU.min).then_inc(s_m, 1)

                def front_r(f):
                    FQ = Q0 + f
                    dve.wait_ge(s_bc1, FQ + 1)
                    nc.vector.tensor_tensor(rbc[:, :], ps[:, SB, :], bc1[:, :],
                                            ALU.subtract).then_inc(s_rbc, 1)

                def front_e(f):
                    dve.wait_ge(s_l, Q0 + f + 1)
                    nc.vector.scalar_tensor_tensor(out=dts[:, :], in0=ps[:, SA, :], scalar=vec("dt_b"), in1=ldt[:, :],
                                                   op0=ALU.add, op1=ALU.max).then_inc(s_dt, 1)

                def first_parts(f):
                    FQ = Q0 + f
                    dve.wait_ge(s_dt, FQ + 1)
                    dve.wait_ge(s_rbc, FQ + 1)
                    dve.wait_ge(s_xcs, FQ + 1)
                    nc.vector.tensor_tensor(us[:, :], dts[:, :], slot(xcs, f), ALU.mult).then_inc(s_parts, 1)
                    if not (isinstance(f, int) and f == 0):
                        dve.wait_ge(s_stk, 16 * 12 * FQ)
                    nc.vector.tensor_copy(part_of("bc", f, 0), bc1[:, :])
                    nc.vector.tensor_copy(part_of("bc", f, 1), rbc[:, :])
                    nc.vector.tensor_copy(part_of("dt", f, 0), dts[:, :])
                    dve.wait_ge(s_parts, FQ * 4 + 1)
                    nc.vector.tensor_copy(part_of("u", f, 0), us[:, :]).then_inc(s_parts, 1)

                def remainders(f):
                    dve.wait_ge(s_parts, (Q0 + f) * 4 + 2)
                    nc.vector.tensor_tensor(rdt[:, :], dts[:, :], part_of("dt", f, 0), ALU.subtract)
                    nc.vector.tensor_tensor(ru[:, :], us[:, :], part_of("u", f, 0), ALU.subtract)
                    nc.vector.tensor_tensor(part_of("bc", f, 2), rbc[:, :], part_of("bc", f, 1),
                                            ALU.subtract).then_inc(s_parts, 1)

                def last_parts(f):
                    dve.wait_ge(s_parts, (Q0 + f) * 4 + 3)
                    nc.vector.tensor_copy(part_of("dt", f, 1), rdt[:, :])
                    nc.vector.tensor_copy(part_of("u", f, 1), ru[:, :]).then_inc(s_parts, 1)
                    dve.wait_ge(s_parts, (Q0 + f) * 4 + 4)
                    nc.vector.tensor_tensor(part_of("dt", f, 2), rdt[:, :], part_of("dt", f, 1), ALU.subtract)
                    nc.vector.tensor_tensor(part_of("u", f, 2), ru[:, :], part_of("u", f, 1),
                                            ALU.subtract).then_inc(s_pcs, 1)

                def scan_group(q, g, first, between=None):
                    Q = Q0 + q
                    for k in range(4):
                        dve.wait_ge(s_uu, Q * 16 + g * 4 + k + 1)
                        if g == 0:
                            dve.wait_ge(s_bcev, Q * 8 + 1 + k)
                        b2 = bsb[:, TC * k:TC * k + TC].rearrange("p (t n) -> p t n", t=2)
                        nc.vector.tensor_tensor(tn(dbx[:, g % 2, :], k),
                                                ps[:, UU + k % 2, :].rearrange("p (t n) -> p t n", t=2),
                                                b2, ALU.mult).then_inc(s_dbx, 1)
                    if between is not None:
                        front_d(between)
                    dve.wait_ge(s_dbx, Q * 16 + g * 4 + 4)
                    dve.wait_ge(s_da, Q * 16 + g * 4 + 4)
                    if g == 0 and first:
                        dve.wait_ge(s_dz, b + 1)
                    if g >= 2:
                        wait_hc(dve, Q, g - 2)
                    elif not first:
                        wait_hc(dve, Q - 1, GR + g - 2)
                    nc.vector.tensor_tensor_scan(hs[:, g % 2, :], dA[:, g % 2, :], dbx[:, g % 2, :], 0.0, ALU.mult,
                                                 ALU.add).then_inc(s_scan, 1)
                    if g in HC_DVE:
                        times_c(dve, nc.vector, Q, g, first, s_hcd)

                def gate(q):
                    Q = Q0 + q
                    dve.wait_ge(s_y, (Q + 1) * GR)
                    nc.vector.scalar_tensor_tensor(
                        out=ya[:, :], in0=slot(xcs, q), scalar=vec("D"), in1=ps[:, YB, :], op0=ALU.mult, op1=ALU.add).then_inc(s_ya, 1)
                    dve.wait_ge(s_ya, Q + 1)
                    dve.wait_ge(s_outp, START + Q)
                    nc.vector.tensor_tensor(ym[:, :], ya[:, :], slot(szs, q), ALU.mult).then_inc(s_ym, 1)

                for f in range(2):
                    front_d(f)
                    front_r(f)
                    front_e(f)
                    if f == 0:
                        first_parts(0)
                        remainders(0)
                        last_parts(0)

                def scan_chunk(q, first, has_front, has_next, has_out):
                    scan_group(q, 0, first)
                    if has_next:
                        first_parts(q + 1)
                        remainders(q + 1)
                        last_parts(q + 1)
                    scan_group(q, 1, first)
                    if not first:
                        gate(q - 1)
                    scan_group(q, 2, first)
                    scan_group(q, 3, first, q + 2 if has_front else None)
                    if has_front:
                        front_r(q + 2)
                        front_e(q + 2)
                mchunks(dve, scan_chunk)
                gate(NQ - 1)

                dve.wait_ge(s_gmm, b + 1)
                nc.vector.tensor_reduce(gs[:, 1:2], ps[:, SB, 0:NQ], AX.X, ALU.add, negate=True).then_inc(s_gmu, 1)
                dve.wait_ge(s_grs, b + 1)
                nc.vector.tensor_scalar(gs[:, 5:6], gs[:, 4:5], vec("gn_w"), None, ALU.mult).then_inc(s_gsc2, 1)
                dve.wait_ge(s_gsc2, b + 1)
                nc.vector.scalar_tensor_tensor(out=gs[:, 6:7], in0=gs[:, 1:2], scalar=gs[:, 5:6], in1=vec("gn_b"),
                                               op0=ALU.mult, op1=ALU.add).then_inc(s_gsc, 1)
                for n in range(4):
                    dve.wait_ge(s_gxp, b * 4 + n + 1)
                    rows = fin[:, 1024 * n:1024 * n + 1024].rearrange("p (r w) -> p r w", r=16)
                    nc.vector.tensor_tensor(rows, rows,
                                            x2[:, 16 * n + 1:16 * n + 17, 1:SIDE + 1], ALU.add).then_inc(s_fin, 1)

        @block.gpsimd
        def _(pool):
            def affine(par, L, norm):
                pool.wait_ge(s_z, L + 1)
                pool.sem_inc(s_seen, 1)
                nc.gpsimd.tensor_scalar(xln[:, par, :], z[:, par, :], vec(f"ln{norm}_w"), vec(f"ln{norm}_b"),
                                        ALU.mult, ALU.add).then_inc(s_xln, 1)
            pool.sem_inc(s_v3, START)
            pool.wait_ge(s_cst, 16)
            def ones(n):
                nc.gpsimd.memset(kst[96:128, :], ROW).then_inc(s_fill, 1)
                pool.wait_ge(s_fill, n + 1)
                pool.sem_inc(s_seen, 1)
                nc.gpsimd.memset(vst[:, :].rearrange("p (n m) -> p n m", m=128)[:, :, 96:128],
                                 1.0).then_inc(s_fill, 1)
            pool.wait_ge(s_prep, 6)
            ones(0)
            pool.wait_ge(s_fill, 2)
            with pool.Fori(0, B) as b:
                L0 = b * 2 * NCH
                affine(0, L0, 1)

                def qkv(i, par, more):
                    G = b * NCH + i
                    if more:
                        affine(1 - par, L0 + i + 1, 1)
                    pool.wait_ge(s_vr, START + G + 1)
                    pool.sem_inc(s_seen, 1)
                    nc.gpsimd.tensor_copy(v_part(1, i), vres4()).then_inc(s_v2, 1)
                    pool.wait_ge(s_v2, G + 1)
                    nc.gpsimd.tensor_tensor(v_part(2, i), vres4(), v_part(1, i), ALU.subtract).then_inc(s_v3, 1)
                chunks(pool, qkv)

                def weights(j, J):
                    pool.wait_ge(s_proj, START + J)
                    pool.sem_inc(s_seen, 1)
                    nc.gpsimd.tensor_copy(pcur[:, :], w("proj")[0:96, ds((j & (NJ - NCH)) * (128 // NCH), 128)]).then_inc(s_pcur, 1)

                def attend(j, first, has_next, has_max):
                    J = b * NJ + j
                    for u in range(UNITS):
                        if u == 1 and not first:
                            weights(j - 1, J - 1)
                        if SUB[u] == "P":
                            pool.wait_ge(s_p32, J * UNITS + u + 1)
                            nc.gpsimd.tensor_tensor(p2[:, u % NB, :], p32[:, u % NB, :], p1[:, u % NB, :],
                                                    ALU.subtract).then_inc(s_subp, 1)
                qchunks(pool, attend)
                weights(NJ - 1, b * NJ + NJ - 1)
                affine(0, L0 + NCH, 2)

                def mlp(i, par, more):
                    if more:
                        affine(1 - par, L0 + NCH + i + 1, 2)
                chunks(pool, mlp)

                pool.wait_ge(s_x2, START + (b + 1) * NCH)
                pool.sem_inc(s_seen, 1)
                nc.gpsimd.memset(dA[:, :, :].rearrange("p a (n t) -> p (a n) t", t=L)[:, :, 0:1], 0.0).then_inc(s_dz, 1)

                def scan_chunk(q, first, has_front, has_next, has_out):
                    for g in range(GR):
                        if g not in HC_DVE:
                            times_c(pool, nc.gpsimd, b * NQ + q, g, first, s_hcp)
                mchunks(pool, scan_chunk)

                pool.wait_ge(s_y, (b + 1) * (NQ * GR))
                pool.sem_inc(s_seen, 1)
                ones(2 * b + 2)
                pool.wait_ge(s_fill, 2 * b + 4)

        @block.sync
        def _(sp):
            sp.dma_start(cst[:, :], consts_in).then_inc(s_cst, 16)
            sp.dma_start(raw[:, :], raw_in).then_inc(s_raw, 16)
            sp.sem_inc(s_out, START)

            def load(b, n):
                rows = x_in[ds(b, 1), :, 16 * n:16 * n + 16, :] if not isinstance(b, int) else \
                    x_in[b:b + 1, :, 16 * n:16 * n + 16, :]
                sp.dma_start(x[:, 1024 * n:1024 * n + 1024],
                             rows.rearrange("a c h w -> c (a h w)")).then_inc(s_x if n else s_x0, 16)
            for n in range(4):
                load(0, n)

            def send_rows(j, J):
                sp.wait_ge(s_clo, J + 1)
                sp.sem_inc(s_step, 1)
                for n, part in enumerate((chi, clo)):
                    dst = qst[96 + n:97 + n, ds(j * TC, TC)]
                    sp.dma_start(dst, part[:, :]).then_inc(s_cdma, 16)

            def send_parts(f, Q0):
                FQ = Q0 + f
                sp.wait_ge(s_pcs, FQ + 1)
                if not (isinstance(f, int) and f < 2):
                    sp.wait_ge(s_uu, (FQ - 1) * 16)
                sp.sem_inc(s_step, 1)
                to = stk.rearrange("p a n -> p (a n)")
                width = len(KINDS) * COLS
                for part in range(PARTS):
                    for t in range(4):
                        dst = to[32 * part:32 * part + 32, ds((f & 1) * width, width)]
                        dst = dst.rearrange("p (h t n) -> p h t n", h=2 * len(KINDS), t=4)[:, :, t, :]
                        src = pcs[32 * t:32 * t + 32, part, :].rearrange("p (h n) -> p h n", h=2 * len(KINDS))
                        sp.dma_start(dst, src).then_inc(s_stk, 16)

            def image(b, last):
                send_rows(0, b * NJ)
                with sp.Fori(1, NJ) as j:
                    send_rows(j, b * NJ + j)
                send_parts(0, b * NQ)
                send_parts(1, b * NQ)
                with sp.Fori(2, NQ) as f:
                    send_parts(f, b * NQ)
                for n in range(4):
                    if not last:
                        sp.wait_ge(s_gxp, 4 * b + n + 1)
                        sp.sem_inc(s_step, 1)
                        load(b + 1, n)
                    sp.wait_ge(s_fin, 4 * b + n + 1)
                    sp.sem_inc(s_step, 1)
                    sp.dma_start(out[ds(b, 1), :, 16 * n:16 * n + 16, :].rearrange("a c h w -> c (a h w)"),
                                 fin[:, 1024 * n:1024 * n + 1024]).then_inc(s_out, 16)
            if B > 1:
                with sp.Fori(0, B - 1) as b:
                    image(b, False)
            image(B - 1, True)
            sp.wait_ge(s_out, START + B * 64)


def layout(inp):
    g = {k: np.asarray(v) for k, v in inp.items()}
    L0 = lambda k: g["L0_conv_" + k]
    parts = {}
    parts["mean"] = np.full((128, 128), 1.0 / C, np.float32)
    parts["ident"] = np.eye(128, dtype=np.float32)
    qkv = L0("qkv_w")
    for n, k in enumerate(("wq", "wk")):
        t = qkv[128 * n:128 * n + 128].T.reshape(C, HEADS, 1, HD)
        parts[k] = np.broadcast_to(t, (C, HEADS, 3, HD)).reshape(C, 384)
    parts["wv"] = qkv[256:384].T
    pw = L0("proj_w").T.reshape(HEADS, HD, C).transpose(1, 0, 2).reshape(1, HD, 512)
    parts["proj"] = np.concatenate([np.broadcast_to(pw, (3, HD, 512)).reshape(96, 512), np.zeros((32, 512), np.float32)])
    parts["spread"] = np.full((128, 128), 1.0 / 32, np.float32)
    parts["head_bias"] = np.stack([L0("proj_b")] + [np.zeros(C, np.float32)] * (HEADS - 1), 1)
    parts["w1"] = L0("fc1_w").T
    parts["w2"] = L0("fc2_w").T.reshape(2, 128, C).transpose(1, 0, 2).reshape(128, 256)
    vec = {k: L0(k) for k in ("ln1_w", "ln1_b", "ln2_w", "ln2_b", "fc2_b")}
    vec["fc1_b0"], vec["fc1_b1"] = L0("fc1_b")[:128], L0("fc1_b")[128:]
    vec["eps"] = np.full(128, EPS, np.float32)
    M = lambda k: g["L1_conv_" + k]
    parts["conv"] = M("conv_w").transpose(1, 2, 3, 0).reshape(C, 9 * C)
    in_w = M("in_proj_w")
    xi, taps, gate = (np.zeros((L, F, L, E), np.float32) for _ in range(3))
    for t in range(L):
        gate[t, :, t, :] = in_w[E:].T
        for k in range(DCONV):
            if t - (DCONV - 1) + k >= 0:
                xi[t - (DCONV - 1) + k, :, t, :] = in_w[:E].T
                taps[t - (DCONV - 1) + k, :, t, :] = M("conv1d_w")[:, 0, k]
    parts["xi"], parts["z"] = xi.reshape(128, 256), gate.reshape(128, 256)
    x_w = M("x_proj_w")
    dt_col, dt_row, bc, o_w = (np.zeros((4, E, 4, n), np.float32) for n in (E, E, 2 * ST_N, F))
    for t in range(4):
        dt_col[t, :, t, :] = x_w[0][:, None]
        dt_row[t, :, t, :] = M("dt_proj_w")[:, 0]
        bc[t, :, t, :] = x_w[1:].T
        o_w[t, :, t, :] = M("out_proj_w").T
    parts["dt"], parts["bc"], parts["out"] = dt_col.reshape(128, 128), bc.reshape(128, 128), o_w.reshape(128, 64)
    row = np.arange(128)
    parts["sum"] = (row % 32 == 8 * (row // 32) + row[:, None] // 16).astype(np.float32)
    n_group = C // GROUPS * N
    parts["group"] = np.where(row[:, None] // 32 == row // 32, np.float32(1.0 / n_group), np.float32(0))
    parts["A"] = M("A_log").reshape(GR, 128).T
    vec.update(conv_b=M("conv_b"), gn_w=M("gn_w"), gn_b=M("gn_b"), conv1d_b=np.tile(M("conv1d_b"), 4),
               dt_b=np.tile(M("dt_proj_b"), 4), D=np.tile(M("D"), 4))
    parts["vecs"] = np.stack([vec[k] for k in VECS], 1)
    wide = np.arange(512)
    of = row[:, None] % 32
    raws = {"conv1d": taps.reshape(128, 256), "dt_row": dt_row.reshape(128, 128),
            "spread_e": of == wide // 16, "spread_b": of == row % 16, "spread_c": of == 16 + row % 16}
    join = lambda d, keys: np.ascontiguousarray(np.concatenate([np.asarray(d[k], np.float32) for k in keys], 1))
    return join(parts, WIDTHS), join(raws, RAW)


def kernel(**inputs):
    import concourse.bacc as bacc
    from concourse.bass_utils import run_bass_kernel_spmd

    nc = bacc.Bacc("TRN2", target_bir_lowering=False, num_devices=1)
    x = np.ascontiguousarray(inputs["x"])
    consts, raws = layout(inputs)
    x_in = nc.dram_tensor("x_in", x.shape, F32, kind="ExternalInput").ap()
    c_in = nc.dram_tensor("consts_in", consts.shape, F32, kind="ExternalInput").ap()
    r_in = nc.dram_tensor("raw_in", raws.shape, F32, kind="ExternalInput").ap()
    out = nc.dram_tensor("out", x.shape, F32, kind="ExternalOutput").ap()
    build(nc, x_in, c_in, r_in, out, x.shape[0])
    r = run_bass_kernel_spmd(nc, [{"x_in": x, "consts_in": consts, "raw_in": raws}], core_ids=[0])
    return r.results[0]["out"]
```

```python
from contextlib import ExitStack

import numpy as np

import concourse.bass as bass
from concourse import mybir

F32 = mybir.dt.float32
F16 = mybir.dt.float16
BF16 = mybir.dt.bfloat16
ALU = mybir.AluOpType
ACT = mybir.ActivationFunctionType
AX = mybir.AxisListType

C = 128
HEADS, HD = 4, 32
SIDE = 64
PAD = SIDE + 2
N = SIDE * SIDE
TC = 512
NCH = N // TC
ROWS = TC // SIDE
NJ = HEADS * NCH
KB = N // 128
UNITS = KB // 2
LAG = 3
NB = 4
TILES = 4 * NCH
EPS = 1e-5
QS = 16.0
SCALE = 1.0 / (QS * QS * float(np.sqrt(HD)))
ROW = 256.0
SHIFT = 14 * float(np.log(2)) / (SCALE * ROW)
SUB = "PPDPPPDPPPDPPPDP"
SUB_LAST = "PDDPDDPDDPDDPDDP"


def upto(table, key, u):
    return sum(t == key for t in table[:u + 1])


def subs_before(b, j, key):
    image = (NJ - 2) * SUB.count(key) + 2 * SUB_LAST.count(key)
    if isinstance(j, int) and j > NJ - 2:
        return b * image + (NJ - 2) * SUB.count(key) + (j - (NJ - 2)) * SUB_LAST.count(key)
    return b * image + j * SUB.count(key)


START = 1
TWO = 2

L, F, E, ST_N, DCONV = 8, 16, 32, 16, 4
NQ = SIDE // 4
SEQ = 2 * C
COLS = L * SEQ
GR = E * ST_N // 128
KINDS = ("bc", "dt", "u")
PARTS = 3
GROUPS = 4

VECS = ["ln1_w", "ln1_b", "ln2_w", "ln2_b", "fc1_b0", "fc1_b1", "fc2_b", "eps",
        "conv_b", "gn_w", "gn_b", "conv1d_b", "dt_b", "D"]
WIDTHS = {"mean": 128, "ident": 128, "wq": 384, "wk": 384, "wv": 128, "proj": 512, "spread": 128, "head_bias": 4,
          "w1": 256, "w2": 256, "vecs": len(VECS), "conv": 9 * 128, "xi": 256, "z": 256, "dt": 128, "bc": 128,
          "out": 64, "sum": 128, "group": 128, "A": GR}
RAW = {"conv1d": 256, "dt_row": 128, "spread_e": 512, "spread_b": 128, "spread_c": 128}


def build(nc, x_in, consts_in, raw_in, out, B):
    at, pos, raw_at, raw_pos = {}, 0, {}, 0
    for k, width in WIDTHS.items():
        at[k] = pos
        pos += width
    for k, width in RAW.items():
        raw_at[k] = raw_pos
        raw_pos += width
    with ExitStack() as ctx:
        sb = lambda name, shape, dt=F32: ctx.enter_context(nc.sbuf_tensor(name, shape, dt))
        sems = lambda names: [ctx.enter_context(nc.semaphore("s_" + name)) for name in names.split()]

        cst = sb("cst", [128, pos])
        x = sb("x", [128, N])
        x2 = sb("x2", [128, PAD, PAD])
        spread = sb("spread_bf", [128, 768], BF16)
        negA = sb("negA", [128, GR])
        ARENA = 149 * 256
        arena = sb("arena", [128, ARENA])
        used = [0]

        def take(shape, dt=F32):
            size = int(np.prod(shape)) // (1 if dt == F32 else 2)
            assert used[0] + size <= ARENA, (used[0] + size, ARENA)
            a = arena[:, used[0]:used[0] + size]
            used[0] += size
            if dt != F32:
                a = a.bitcast(dt)
            if len(shape) == 2:
                a = a.rearrange("p (a b) -> p a b", a=shape[0])
            elif len(shape) == 3:
                a = a.rearrange("p (a b c) -> p a b c", a=shape[0], b=shape[1])
            return a

        qst = take([HEADS * N], F16)
        kst = take([HEADS * N], F16)
        vst = take([HEADS * KB * 128], BF16)
        at_p = used[0]
        p32 = take([NB, 1024])
        p1 = p32.rearrange("p b n -> p (b n)").bitcast(BF16).rearrange("p (b n e) -> p b n e", b=NB, e=2)[:, :, :, 1]
        p2 = take([NB, 1024], F16)
        osb, lns, rcp = take([TC]), take([TC]), take([TC])
        onrm = take([TC])[0:96, :]
        mx, cneg = take([TILES]), take([4])
        crow = take([128])[0:4, :]
        chi, clo = take([128], F16)[0:4, :], take([128], F16)[0:4, :]
        pcur = take([128])[0:96, :]
        used[0] = at_p
        xc, sq, rstd, z, xln = (take([2, TC]) for _ in range(5))
        lnv, vres = take([TC]), take([TC])
        at_final = used[0]
        used[0] = 0
        xln2, hid = take([N]), take([4, TC])
        used[0] = 0
        dA, dbx = take([2, COLS]), take([2, COLS])
        hs = take([2, COLS])
        hC = take([2, COLS])
        bsb, csb = take([COLS]), take([COLS])
        stk = take([2, len(KINDS) * COLS], BF16)
        pcs = take([PARTS, len(KINDS) * TC], BF16)
        bc1 = take([TC], BF16)
        yc, yT = take([SEQ]), take([SEQ])
        xcs, szs = take([4, TC]), take([4, TC])
        mdt, dts, us, rbc, rdt, ru, ya, ym = (take([TC]) for _ in range(8))
        edt = ldt = mdt
        gs, gsums = take([8]), take([NQ])
        used[0] = 0
        raw = take([raw_pos])
        used[0] = at_final
        fin = take([N])
        xr = x
        ps = ctx.enter_context(nc.psum_tensor("ps", [128, 8, TC], F32))

        w = lambda k: cst[:, at[k]:at[k] + WIDTHS[k]]
        vec = lambda k: cst[:, at["vecs"] + VECS.index(k):at["vecs"] + VECS.index(k) + 1]

        s_cst, s_raw, s_x0, s_x, s_out = sems("cst raw x0 x out")
        s_prep, s_fill, s_dz = sems("prep fill dz")
        s_mean, s_xc, s_sq, s_var, s_ln, s_rstd, s_z, s_xln = sems("mean xc sq var ln rstd z xln")
        s_qk, s_q1, s_q2, s_v, s_v1, s_vr, s_v2, s_v3 = sems("qk q1 q2 v v1 vr v2 v3")
        s_sm, s_red, s_cneg, s_ct, s_chi, s_clo, s_cdma = sems("sm red cneg ct chi clo cdma")
        s_st, s_p32, s_subp, s_subd, s_pv, s_oev = sems("st p32 subp subd pv oev")
        s_lns, s_rcp, s_bc, s_on, s_pcur, s_proj, s_tbfree = sems("lns rcp bc on pcur proj tbfree")
        s_fc1, s_gelu, s_fc2, s_x2 = sems("fc1 gelu fc2 x2")
        s_conv, s_yc, s_tr, s_yT, s_xi, s_zz, s_xcs, s_szs = sems("conv yc tr yT xi zz xcs szs")
        s_dtp, s_bcp, s_bc1, s_rbc, s_m, s_e, s_l, s_dt = sems("dtp bcp bc1 rbc m e l dt")
        s_parts, s_pcs, s_stk = sems("parts pcs stk")
        s_bcu, s_bcev, s_dtu, s_uu, s_da, s_dbx, s_scan, s_hc, s_hcd, s_y = sems("bcu bcev dtu uu da dbx scan hc hcd y")
        s_ya, s_ym, s_outp, s_xr = sems("ya ym outp xr")
        s_gmm, s_gmu, s_gsq, s_gvv, s_gln, s_grs, s_gsc2, s_gsc, s_gxp, s_fin = sems("gmm gmu gsq gvv gln grs gsc2 gsc gxp fin")
        s_seen, s_step = sems("seen step")

        MEAN, VAR, QK, VB = 0, 1, 2, 6
        ST, SM, OB, TB = 0, 4, 6, 7
        FC1, FC2 = 2, 6
        DT, UU, CB, YB, SA, SB = 0, 2, 4, 5, 6, 7

        block = ctx.enter_context(nc.Block())
        ds = bass.ds

        def slot(t, f):
            return t.rearrange("p a b -> p (a b)")[:, ds((f & 3) * TC, TC)]

        def part_of(what, part):
            return pcs[:, part, TC * KINDS.index(what):TC * KINDS.index(what) + TC]

        def stack(what, q, n):
            at = KINDS.index(what) * COLS + n * TC
            return stk.rearrange("p a n -> p (a n)")[0:96, ds((q & 1) * (len(KINDS) * COLS) + at, TC)]

        def states_times_c(api, g):
            return api.tensor_tensor(hC[:, g % 2, :].rearrange("p (t n) -> p t n", t=L),
                                     hs[:, g % 2, :].rearrange("p (n t) -> p t n", t=L),
                                     csb[:, :].rearrange("p (t n) -> p t n", t=L), ALU.mult)

        def v_psum():
            return ps[:, VB, :].rearrange("p (k h d) -> p k h d", k=4, h=HEADS)

        def v_part(part, i):
            v = vst[:, :].rearrange("p (h k m) -> p k h m", h=HEADS, k=KB)
            return v[:, ds(i * 4, 4), :, HD * part:HD * part + HD]

        def vres4():
            return vres[:, :].rearrange("p (k h d) -> p k h d", k=4, h=HEADS)

        def head_base(j):
            return (j & (NJ - NCH)) * TC

        def chunks(eng, body):
            with eng.Fori(0, NCH // 2 - 1) as t:
                body(2 * t, 0, True)
                body(2 * t + 1, 1, True)
            body(NCH - 2, 0, True)
            body(NCH - 1, 1, False)

        def mchunks(eng, body):
            body(0, True, True, True, False)
            body(1, False, True, True, False)
            with eng.Fori(0, NQ - 4) as t:
                body(t + 2, False, True, True, True)
            body(NQ - 2, False, False, True, True)
            body(NQ - 1, False, False, False, True)

        def tn(t, k):
            return t.rearrange("p (n t) -> p t n", t=L)[:, 2 * k:2 * k + 2, :]

        def nt(t, k):
            return t.rearrange("p (h t n) -> p t h n", h=2, t=4)[:, k, :, :]

        def qchunks(eng, body):
            body(0, True, True, True)
            with eng.Fori(0, NJ - 3) as t:
                body(t + 1, False, True, True)
            body(NJ - 2, False, True, False)
            body(NJ - 1, False, False, False)

        @block.tensor
        def _(pe):
            def mean(i, L):
                pe.wait_ge(s_xc, START + L)
                nc.tensor.matmul(ps[:, MEAN, :], w("mean"), x[:, ds(i * TC, TC)],
                                 start=True, stop=True).then_inc(s_mean, 1)

            def var(par, L):
                pe.wait_ge(s_sq, L + 1)
                pe.wait_ge(s_ln, START + L)
                nc.tensor.matmul(ps[:, VAR, :], w("mean"), sq[:, par, :],
                                 start=True, stop=True).then_inc(s_var, 1)

            def project(par, K, which):
                for h in range(HEADS):
                    k = h + (HEADS if which == "wk" else 0)
                    pe.wait_ge(s_q2, K + k + 1)
                    nc.tensor.matmul(ps[0:96, QK + h, :], w(which)[:, 96 * h:96 * h + 96], xln[:, par, :],
                                     start=True, stop=True).then_inc(s_qk, 1)

            pe.wait_ge(s_cst, 16)
            pe.wait_ge(s_prep, 6)
            pe.sem_inc(s_pv, NB)
            for q in (s_proj, s_fc2, s_outp):
                pe.sem_inc(q, START)
            pe.sem_inc(s_fc2, TWO - START)
            with pe.Fori(0, B) as b:
                pe.wait_ge(s_x0, (b + 1) * 16)
                L0 = b * 2 * NCH
                mean(0, L0)
                var(0, L0)

                def qkv(i, par, more):
                    K = (b * NCH + i) * 2 * HEADS
                    if more:
                        pe.wait_ge(s_x, (b + 1) * 48)
                        mean(i + 1, L0 + i + 1)
                    pe.wait_ge(s_xln, L0 + i + 1)
                    project(par, K, "wq")
                    if more:
                        var(1 - par, L0 + i + 1)
                    project(par, K, "wk")
                    pe.wait_ge(s_vr, START + b * NCH + i)
                    for t in range(4):
                        mm = nc.tensor.matmul(ps[:, VB, 128 * t:128 * t + 128], xln[:, par, 128 * t:128 * t + 128],
                                              w("wv"), start=True, stop=True)
                    mm.then_inc(s_v, 1)
                chunks(pe, qkv)

                def max_tile(j, m, head):
                    pe.wait_ge(s_red, (b * NJ + j) * TILES + m + 1)
                    nc.tensor.matmul(ps[:, SM + m % 2, :], qst[0:96, ds(j * TC + m // NCH * 128, 128)],
                                     kst[0:96, ds(head + m % NCH * TC, TC)],
                                     start=True, stop=True).then_inc(s_sm, 1)

                def scores(j, u, head):
                    if not (isinstance(j, int) and j == 0 and u < 2):
                        pe.wait_ge(s_p32, (b * NJ + j) * UNITS + u - 1)
                    if u == 0:
                        pe.wait_ge(s_cdma, 32 * (b * NJ + j + 1))
                    for t in range(2):
                        mm = nc.tensor.matmul(ps[:, ST + 2 * (u % 2) + t, :],
                                              kst[0:98, ds(head + (2 * u + t) * 128, 128)],
                                              qst[0:98, ds(j * TC, TC)], start=True, stop=True)
                    mm.then_inc(s_st, 1)

                def pv(j, u, head):
                    J = b * NJ + j
                    table = SUB_LAST if isinstance(j, int) and j >= NJ - 2 else SUB
                    if table[u] == "P":
                        pe.wait_ge(s_subp, subs_before(b, j, "P") + upto(table, "P", u))
                    else:
                        pe.wait_ge(s_subd, subs_before(b, j, "D") + upto(table, "D", u))
                    if u == 0:
                        pe.wait_ge(s_oev, START + J)
                    for t in range(2):
                        for n, part in enumerate((p1, p2)):
                            mm = nc.tensor.matmul(ps[:, OB, :], vst[:, ds(head + (2 * u + t) * 128, 128)],
                                                  part[:, u % NB, TC * t:TC * t + TC],
                                                  start=(u == 0 and t == 0 and n == 0),
                                                  stop=(u == UNITS - 1 and t == 1 and n == 1))
                    mm.then_inc(s_pv, 1)

                def turn_max(idx, J):
                    pe.wait_ge(s_cneg, J + 1)
                    pe.wait_ge(s_tbfree, b * 3 * NJ + idx + 1)
                    nc.tensor.transpose(ps[0:4, TB, 0:128], cneg[:, :], w("ident")).then_inc(s_ct, 1)

                def spread_sums(idx, J):
                    pe.wait_ge(s_rcp, J + 1)
                    pe.wait_ge(s_tbfree, b * 3 * NJ + idx + 1)
                    nc.tensor.matmul(ps[0:96, TB, :], w("spread")[96:128, 0:96], rcp[96:128, :],
                                     start=True, stop=True).then_inc(s_bc, 1)

                def out_project(idx, J):
                    pe.wait_ge(s_on, START + J + 1)
                    pe.wait_ge(s_pcur, J + 1)
                    pe.wait_ge(s_tbfree, b * 3 * NJ + idx + 1)
                    nc.tensor.matmul(ps[:, TB, :], pcur[:, :], onrm[:, :],
                                     start=True, stop=True).then_inc(s_proj, 1)

                pe.wait_ge(s_fill, 2 * b + 2)
                pe.wait_ge(s_q2, 4 + (b + 1) * NCH * 2 * HEADS)
                for m in range(TILES):
                    max_tile(0, m, 0)
                turn_max(0, b * NJ)
                for m in range(TILES):
                    max_tile(1, m, 0)
                pe.wait_ge(s_v3, START + (b + 1) * NCH)
                for u in range(LAG):
                    scores(0, u, 0)

                def attend(j, first, has_next, has_max):
                    J = b * NJ + j
                    base = 2 + 3 * (j - 1) if not first else 1
                    for u in range(UNITS):
                        if u + LAG < UNITS:
                            scores(j, u + LAG, head_base(j))
                        elif has_next:
                            scores(j + 1, u + LAG - UNITS, head_base(j + 1))
                        if has_max:
                            for m in (2 * u, 2 * u + 1):
                                max_tile(j + 2, m, head_base(j + 2))
                        pv(j, u, head_base(j))
                        if u == 1 and has_next:
                            turn_max(base, J + 1)
                        if u == 4 and not first:
                            spread_sums(base + has_next, J - 1)
                        if u == 8 and not first:
                            out_project(base + has_next + 1, J - 1)
                qchunks(pe, attend)
                spread_sums(3 * NJ - 2, b * NJ + NJ - 1)
                out_project(3 * NJ - 1, b * NJ + NJ - 1)

                pe.wait_ge(s_tbfree, 1 + (b + 1) * 3 * NJ)
                L2 = L0 + NCH
                mean(0, L2)

                def norm2(i, par, more):
                    if more:
                        mean(i + 1, L2 + i + 1)
                    var(par, L2 + i)
                chunks(pe, norm2)

                G0 = b * NCH

                def fc1(i, par):
                    G = G0 + i
                    pe.wait_ge(s_xln, L2 + i + 1)
                    pe.wait_ge(s_gelu, 2 * G + START)
                    for n in range(2):
                        nc.tensor.matmul(ps[:, FC1 + 2 * par + n, :], w("w1")[:, 128 * n:128 * n + 128],
                                         xln2[:, ds(i * TC, TC)], start=True, stop=True).then_inc(s_fc1, 1)
                fc1(0, 0)

                def mlp(i, par, more):
                    G = G0 + i
                    if more:
                        fc1(i + 1, 1 - par)
                    pe.wait_ge(s_gelu, 2 * G + 2 + START + 2)
                    pe.wait_ge(s_x2, START + G)
                    for n in range(2):
                        mm = nc.tensor.matmul(ps[:, FC2, :], w("w2")[:, 128 * n:128 * n + 128],
                                              hid[:, 2 * par + n, :], start=(n == 0), stop=(n == 1))
                    mm.then_inc(s_fc2, 1)
                chunks(pe, mlp)

                Q0 = b * NQ

                def conv(f, half):
                    if half == 0:
                        if not isinstance(f, int):
                            pe.wait_ge(s_xr, START + Q0 + f - 3)
                        if not (isinstance(f, int) and f == 0):
                            pe.wait_ge(s_dt, Q0 + f)
                    for n in range(5) if half == 0 else range(5, 9):
                        rows = x2[:, ds(4 * f + n // 3, 4), n % 3:n % 3 + SIDE]
                        mm = nc.tensor.matmul(ps[:, SA, 0:SEQ].rearrange("p (r w) -> p r w", r=4),
                                              w("conv")[:, 128 * n:128 * n + 128], rows,
                                              start=(n == 0), stop=(n == 8))
                    if half == 1:
                        mm.then_inc(s_conv, 1)

                def turn(f):
                    pe.wait_ge(s_yc, Q0 + f + 1)
                    if not (isinstance(f, int) and f == 0):
                        pe.wait_ge(s_rbc, Q0 + f)
                    for r in range(2):
                        mm = nc.tensor.transpose(ps[:, SB, C * r:C * r + C], yc[:, C * r:C * r + C], w("ident"))
                    mm.then_inc(s_tr, 1)

                def in_project(f):
                    pe.wait_ge(s_yT, Q0 + f + 1)
                    for k, bank, s_k in (("xi", SA, s_xi), ("z", SB, s_zz)):
                        for n in range(2):
                            mm = nc.tensor.matmul(ps[:, bank, SEQ * n:SEQ * n + SEQ],
                                                  w(k)[:, 128 * n:128 * n + 128], yT[:, :], start=True, stop=True)
                        mm.then_inc(s_k, 1)

                def x_project(f):
                    pe.wait_ge(s_xcs, Q0 + f + 1)
                    pe.wait_ge(s_szs, Q0 + f + 1)
                    nc.tensor.matmul(ps[:, SA, :], w("dt"), slot(xcs, f), start=True, stop=True).then_inc(s_dtp, 1)
                    nc.tensor.matmul(ps[:, SB, :], w("bc"), slot(xcs, f), start=True, stop=True).then_inc(s_bcp, 1)

                def spread_bc(q, n):
                    sel = spread[0:96, 512 + 128 * (n // 4):640 + 128 * (n // 4)]
                    nc.tensor.matmul(ps[:, n if n < 4 else CB, :], sel, stack("bc", q, n % 4),
                                     start=True, stop=True).then_inc(s_bcu, 1)

                def spread_b(q, first):
                    Q = Q0 + q
                    pe.wait_ge(s_stk, 16 * 12 * (Q + 1))
                    for n in range(4):
                        if n == 0 and not first:
                            pe.wait_ge(s_da, Q * 16)
                        if n == 2 and not first:
                            pe.wait_ge(s_dbx, Q * 16)
                        spread_bc(q, n)

                def spread_c(q, n):
                    pe.wait_ge(s_bcev, (Q0 + q) * 8 + n)
                    spread_bc(q, n)

                def spread_group(q, g, which):
                    Q = Q0 + q
                    sel = spread[0:96, 128 * g:128 * g + 128]
                    for k in which:
                        n = Q * 16 + g * 4 + k
                        if g == 0 and k < 2:
                            pe.wait_ge(s_bcev, Q * 8 + 1 + k)
                        else:
                            pe.wait_ge(s_da, n - 1)
                        nc.tensor.matmul(ps[:, DT + k % 2, :], sel, stack("dt", q, k),
                                         start=True, stop=True).then_inc(s_dtu, 1)
                        if g == 0 and k < 2:
                            pe.wait_ge(s_bcev, Q * 8 + 3 + k)
                        else:
                            pe.wait_ge(s_dbx, n - 1)
                        nc.tensor.matmul(ps[:, UU + k % 2, :], sel, stack("u", q, k),
                                         start=True, stop=True).then_inc(s_uu, 1)

                def sum_states(q, g, first):
                    Q = Q0 + q
                    if isinstance(q, int) and q == NQ - 1 and g == GR - 1:
                        pe.wait_ge(s_hcd, b + 1)
                    else:
                        pe.wait_ge(s_hc, Q * GR + g + 1)
                    if g == 0 and not first:
                        pe.wait_ge(s_ya, Q)
                    for t in range(4):
                        mm = nc.tensor.matmul(ps[32 * t:32 * t + 32, YB, :], w("sum")[:, 32 * g:32 * g + 32],
                                              nt(hC[:, g % 2, :], t), start=(g == 0), stop=(g == GR - 1))
                    mm.then_inc(s_y, 1)

                def out_project(q, fronts):
                    pe.wait_ge(s_ym, START + Q0 + q + 1)
                    pe.wait_ge(s_dt, Q0 + fronts)
                    pe.wait_ge(s_xr, START + Q0 + q)
                    for r in range(2):
                        for n in range(2):
                            mm = nc.tensor.matmul(ps[:, SA, 128 * r + 64 * n:128 * r + 64 * n + 64],
                                                  ym[:, SEQ * n + C * r:SEQ * n + C * r + C], w("out"),
                                                  start=True, stop=True)
                    mm.then_inc(s_outp, 1)

                pe.wait_ge(s_x2, START + (b + 1) * NCH)
                for f in range(2):
                    conv(f, 0)
                    conv(f, 1)
                    turn(f)
                    in_project(f)
                    x_project(f)

                def scan_chunk(q, first, has_front, has_next, has_out):
                    fronts = q + 2 if has_front else NQ
                    spread_b(q, first)
                    spread_group(q, 0, (0,))
                    spread_group(q, 0, (1,))
                    if not first:
                        sum_states(q - 1, 2, False)
                    if has_out:
                        out_project(q - 2, fronts)
                    spread_group(q, 0, (2,))
                    spread_group(q, 0, (3,))
                    spread_c(q, 4)
                    spread_c(q, 5)
                    if has_front:
                        conv(q + 2, 0)
                    spread_group(q, 1, (0,))
                    spread_c(q, 6)
                    spread_group(q, 1, (1,))
                    spread_c(q, 7)
                    if has_front:
                        conv(q + 2, 1)
                    spread_group(q, 1, (2,))
                    spread_group(q, 1, (3,))
                    if not first:
                        sum_states(q - 1, 3, False)
                    if has_front:
                        turn(q + 2)
                    spread_group(q, 2, (0,))
                    spread_group(q, 2, (1,))
                    if has_front:
                        in_project(q + 2)
                    spread_group(q, 2, (2,))
                    spread_group(q, 2, (3,))
                    sum_states(q, 0, first)
                    spread_group(q, 3, (0,))
                    spread_group(q, 3, (1,))
                    if has_front:
                        x_project(q + 2)
                    spread_group(q, 3, (2,))
                    spread_group(q, 3, (3,))
                    sum_states(q, 1, first)
                mchunks(pe, scan_chunk)
                out_project(NQ - 2, NQ)
                sum_states(NQ - 1, 2, False)
                sum_states(NQ - 1, 3, False)
                out_project(NQ - 1, NQ)

                pe.wait_ge(s_xr, START + (b + 1) * NQ)
                nc.tensor.matmul(ps[:, SB, 0:NQ], w("group"), gsums[:, :], start=True, stop=True).then_inc(s_gmm, 1)
                pe.wait_ge(s_gsq, b + 1)
                nc.tensor.matmul(ps[:, SB, 0:1], w("group"), gs[:, 2:3], start=True, stop=True).then_inc(s_gvv, 1)

        @block.scalar
        def _(act):
            def square(par, L):
                act.wait_ge(s_xc, START + L + 1)
                nc.scalar.activation(sq[:, par, :], xc[:, par, :], ACT.Square).then_inc(s_sq, 1)

            def inverse_deviation(par, L):
                act.wait_ge(s_var, L + 1)
                nc.scalar.activation(lnv[:, :], ps[:, VAR, :], ACT.Ln, bias=vec("eps")).then_inc(s_ln, 1)
                act.wait_ge(s_ln, START + L + 1)
                nc.scalar.activation(rstd[:, par, :], lnv[:, :], ACT.Exp, scale=-0.5).then_inc(s_rstd, 1)

            act.wait_ge(s_cst, 16)
            for q in (s_ln, s_oev, s_gelu, s_xr):
                act.sem_inc(q, START)
            act.sem_inc(s_gelu, 2)
            act.wait_ge(s_raw, 16)
            nc.scalar.activation(spread[:, :], raw[:, raw_at["spread_e"]:raw_at["spread_e"] + 768],
                                 ACT.Copy).then_inc(s_prep, 1)
            nc.scalar.activation(negA[:, :], w("A"), ACT.Exp).then_inc(s_prep, 1)
            act.wait_ge(s_prep, 6)
            with act.Fori(0, B) as b:
                L0 = b * 2 * NCH
                nc.scalar.preload_act_table_set("natural_log_exp_and_others")
                square(0, L0)
                inverse_deviation(0, L0)

                def qkv(i, par, more):
                    L = L0 + i
                    K = (b * NCH + i) * 2 * HEADS
                    if more:
                        square(1 - par, L + 1)
                    for k in range(2 * HEADS):
                        if k == HEADS and more:
                            inverse_deviation(1 - par, L + 1)
                        act.wait_ge(s_qk, K + k + 1)
                        st = qst if k < HEADS else kst
                        h = k % HEADS
                        nc.scalar.activation(st[0:96, ds(i * TC + h * N, TC)], ps[0:96, QK + h, :],
                                             ACT.Copy, scale=QS).then_inc(s_q1, 1)
                    act.wait_ge(s_v, b * NCH + i + 1)
                    nc.scalar.activation(v_part(0, i), v_psum(), ACT.Copy).then_inc(s_v1, 1)
                chunks(act, qkv)

                def attend(j, first, has_next, has_max):
                    J = b * NJ + j
                    for u in range(UNITS):
                        n = J * UNITS + u
                        act.wait_ge(s_st, n + 1)
                        act.wait_ge(s_pv, n + 1)
                        src = ps[:, ST + 2 * (u % 2):ST + 2 * (u % 2) + 2, :]
                        nc.scalar.activation(p32[:, u % NB, :], src, ACT.Exp, scale=SCALE).then_inc(s_p32, 1)
                        if u < 4 and not first:
                            read_sums(J - 1, u)

                def read_sums(J, u):
                    if u == 1:
                        copy_sums(J)
                    elif u == 2:
                        act.wait_ge(s_oev, START + J + 1)
                        nc.scalar.activation(lns[96:128, :], osb[96:128, :], ACT.Ln).then_inc(s_lns, 1)
                    elif u == 3:
                        act.wait_ge(s_lns, J + 1)
                        nc.scalar.activation(rcp[96:128, :], lns[96:128, :], ACT.Exp, scale=-1.0).then_inc(s_rcp, 1)

                def copy_sums(J):
                    act.wait_ge(s_pv, NB + (J + 1) * UNITS)
                    act.wait_ge(s_on, START + J)
                    nc.scalar.activation(osb[:, :], ps[:, OB, :], ACT.Copy).then_inc(s_oev, 1)
                nc.scalar.preload_act_table_set("natural_log_exp_and_others")
                qchunks(act, attend)
                for u in range(1, 4):
                    read_sums(b * NJ + NJ - 1, u)

                L2 = L0 + NCH
                square(0, L2)

                def norm2(i, par, more):
                    if more:
                        square(1 - par, L2 + i + 1)
                    act.wait_ge(s_rstd, L2 + i)
                    inverse_deviation(par, L2 + i)
                chunks(act, norm2)
                nc.scalar.preload_act_table(ACT.Gelu)

                def mlp(i, par, more):
                    G = b * NCH + i
                    act.wait_ge(s_fc2, START + G)
                    for n in range(2):
                        act.wait_ge(s_fc1, 2 * G + n + 1)
                        nc.scalar.activation(hid[:, 2 * par + n, :], ps[:, FC1 + 2 * par + n, :], ACT.Gelu,
                                             bias=vec(f"fc1_b{n}")).then_inc(s_gelu, 1)
                chunks(act, mlp)

                Q0 = b * NQ

                def front_a(f):
                    act.wait_ge(s_conv, Q0 + f + 1)
                    nc.scalar.activation(yc[:, :], ps[:, SA, 0:SEQ], ACT.Identity, bias=vec("conv_b")).then_inc(s_yc, 1)

                def front_b(f):
                    act.wait_ge(s_tr, Q0 + f + 1)
                    nc.scalar.activation(yT[:, :], ps[:, SB, 0:SEQ], ACT.Copy).then_inc(s_yT, 1)

                def front_silu(f):
                    act.wait_ge(s_xi, Q0 + f + 1)
                    if not isinstance(f, int):
                        act.wait_ge(s_ym, START + Q0 + f - 3)
                    nc.scalar.activation(slot(xcs, f), ps[:, SA, :], ACT.Silu, bias=vec("conv1d_b")).then_inc(s_xcs, 1)
                    act.wait_ge(s_zz, Q0 + f + 1)
                    nc.scalar.activation(slot(szs, f), ps[:, SB, :], ACT.Silu).then_inc(s_szs, 1)
                    nc.scalar.preload_act_table_set("natural_log_exp_and_others")

                def front_c(f):
                    act.wait_ge(s_bcp, Q0 + f + 1)
                    if not (isinstance(f, int) and f == 0):
                        act.wait_ge(s_parts, (Q0 + f) * 4 - 2)
                    nc.scalar.activation(bc1[:, :], ps[:, SB, :], ACT.Copy).then_inc(s_bc1, 1)

                def front_s(f):
                    act.wait_ge(s_m, Q0 + f + 1)
                    nc.scalar.activation(edt[:, :], mdt[:, :], ACT.Exp).then_inc(s_e, 1)
                    act.wait_ge(s_e, Q0 + f + 1)
                    nc.scalar.activation(ldt[:, :], edt[:, :], ACT.Ln, bias=1.0).then_inc(s_l, 1)

                def copy_bc(q, first, which):
                    Q = Q0 + q
                    for n in which:
                        if n == 0 and not first:
                            act.wait_ge(s_dbx, Q * 16)
                        if n == 4 and not first:
                            act.wait_ge(s_hc, Q * GR)
                        act.wait_ge(s_bcu, Q * 8 + n + 1)
                        bank = n if n < 4 else CB
                        dst = (bsb if n < 4 else csb)[:, TC * (n % 4):TC * (n % 4) + TC]
                        nc.scalar.activation(dst, ps[:, bank, :], ACT.Copy).then_inc(s_bcev, 1)

                def decays(q, g, which, first):
                    Q = Q0 + q
                    if 0 in which and not (first and g < 2):
                        act.wait_ge(s_scan, Q * GR + g - 1)
                    for k in which:
                        act.wait_ge(s_dtu, Q * 16 + g * 4 + k + 1)
                        lo = 1 if k == 0 else 0
                        src = ps[:, DT + k % 2, :].rearrange("p (t n) -> p t n", t=2)[:, lo:2, :]
                        nc.scalar.activation(tn(dA[:, g % 2, :], k)[:, lo:2, :], src, ACT.Exp,
                                             scale=negA[:, g:g + 1]).then_inc(s_da, 1)

                def out_rows(q):
                    act.wait_ge(s_outp, START + Q0 + q + 1)
                    nc.scalar.activation(xr[:, ds(q * SEQ, SEQ)], ps[:, SA, 0:SEQ], ACT.Copy,
                                         accum_out=gsums[:, ds(q, 1)]).then_inc(s_xr, 1)

                for f in range(2):
                    front_a(f)
                    front_b(f)
                    front_silu(f)
                    front_c(f)
                    front_s(f)

                def scan_chunk(q, first, has_front, has_next, has_out):
                    copy_bc(q, first, range(4))
                    decays(q, 0, (0,), first)
                    decays(q, 0, (1,), first)
                    if has_out:
                        out_rows(q - 2)
                    decays(q, 0, (2,), first)
                    decays(q, 0, (3,), first)
                    copy_bc(q, first, (4,))
                    copy_bc(q, first, (5,))
                    decays(q, 1, (0,), first)
                    copy_bc(q, first, (6,))
                    decays(q, 1, (1,), first)
                    copy_bc(q, first, (7,))
                    if has_front:
                        front_a(q + 2)
                    decays(q, 1, (2,), first)
                    decays(q, 1, (3,), first)
                    if has_front:
                        front_b(q + 2)
                    decays(q, 2, (0,), first)
                    decays(q, 2, (1,), first)
                    decays(q, 2, (2,), first)
                    decays(q, 2, (3,), first)
                    if has_front:
                        front_silu(q + 2)
                    decays(q, 3, (0,), first)
                    decays(q, 3, (1,), first)
                    decays(q, 3, (2,), first)
                    decays(q, 3, (3,), first)
                    if has_front:
                        front_c(q + 2)
                        front_s(q + 2)
                mchunks(act, scan_chunk)
                out_rows(NQ - 2)
                out_rows(NQ - 1)

                nc.scalar.preload_act_table_set("natural_log_exp_and_others")
                act.wait_ge(s_xr, START + Q0 + NQ)
                act.wait_ge(s_gmu, b + 1)
                nc.scalar.activation(fin[:, :], xr[:, :], ACT.Square, bias=gs[:, 1:2],
                                     accum_out=gs[:, 2:3]).then_inc(s_gsq, 1)
                act.wait_ge(s_gvv, b + 1)
                nc.scalar.activation(gs[:, 3:4], ps[:, SB, 0:1], ACT.Ln, bias=vec("eps")).then_inc(s_gln, 1)
                act.wait_ge(s_gln, b + 1)
                nc.scalar.activation(gs[:, 4:5], gs[:, 3:4], ACT.Exp, scale=-0.5).then_inc(s_grs, 1)
                act.wait_ge(s_gsc, b + 1)
                for n in range(4):
                    nc.scalar.activation(fin[:, 1024 * n:1024 * n + 1024], xr[:, 1024 * n:1024 * n + 1024], ACT.Silu,
                                         scale=gs[:, 5:6], bias=gs[:, 6:7]).then_inc(s_gxp, 1)

        @block.vector
        def _(dve):
            def centre(i, par, L):
                dve.wait_ge(s_mean, L + 1)
                nc.vector.tensor_tensor(xc[:, par, :], x[:, ds(i * TC, TC)], ps[:, MEAN, :],
                                        ALU.subtract).then_inc(s_xc, 1)

            def normalise(par, L):
                dve.wait_ge(s_rstd, L + 1)
                nc.vector.tensor_tensor(z[:, par, :], xc[:, par, :], rstd[:, par, :], ALU.mult).then_inc(s_z, 1)

            dve.sem_inc(s_q2, 4)
            dve.sem_inc(s_red, 2)
            dve.sem_inc(s_tbfree, 1)
            for q in (s_xc, s_vr, s_on, s_x2, s_ym):
                dve.sem_inc(q, START)
            dve.wait_ge(s_cst, 16)
            dve.wait_ge(s_raw, 16)
            r = lambda k: raw[:, raw_at[k]:raw_at[k] + RAW[k]]
            nc.vector.memset(x2[:, :, :], 0.0).then_inc(s_prep, 1)
            nc.vector.tensor_tensor(w("xi"), w("xi"), r("conv1d"), ALU.mult).then_inc(s_prep, 1)
            nc.vector.tensor_tensor(w("dt"), w("dt"), r("dt_row"), ALU.mult).then_inc(s_prep, 1)
            dve.wait_ge(s_prep, 5)
            nc.vector.tensor_scalar(negA[:, :], negA[:, :], -1.0, None, ALU.mult).then_inc(s_prep, 1)
            dve.wait_ge(s_prep, 6)
            with dve.Fori(0, B) as b:
                L0 = b * 2 * NCH
                centre(0, 0, L0)
                normalise(0, L0)

                def qkv(i, par, more):
                    L = L0 + i
                    K = (b * NCH + i) * 2 * HEADS
                    if more:
                        centre(i + 1, 1 - par, L + 1)
                    for k in range(2 * HEADS):
                        if k == HEADS and more:
                            normalise(1 - par, L + 1)
                        dve.wait_ge(s_q1, K + k + 1)
                        st, r = (qst, 64) if k < HEADS else (kst, 32)
                        h = k % HEADS
                        low = st[r:r + 32, ds(i * TC + h * N, TC)]
                        nc.vector.scalar_tensor_tensor(out=low, in0=ps[r:r + 32, QK + h, :], scalar=QS, in1=low,
                                                       op0=ALU.mult, op1=ALU.subtract).then_inc(s_q2, 1)
                    dve.wait_ge(s_v1, b * NCH + i + 1)
                    dve.wait_ge(s_v3, START + b * NCH + i)
                    nc.vector.tensor_tensor(vres4(), v_psum(), v_part(0, i), ALU.subtract).then_inc(s_vr, 1)
                chunks(dve, qkv)

                def reduce_tile(j, m):
                    T = (b * NJ + j) * TILES + m
                    dve.wait_ge(s_sm, T + 1)
                    nc.vector.tensor_reduce(mx[:, m:m + 1], ps[:, SM + m % 2, :], AX.X,
                                            ALU.max).then_inc(s_red, 1)

                def chunk_max(J):
                    dve.wait_ge(s_red, 2 + (J + 1) * TILES)
                    nc.vector.tensor_reduce(cneg[:, :], mx[:, :].rearrange("p (q t) -> p q t", q=4), AX.X,
                                            ALU.max, negate=True).then_inc(s_cneg, 1)

                def max_rows(J, first=False):
                    dve.wait_ge(s_ct, J + 1)
                    nc.vector.tensor_scalar(crow[:, :], ps[0:4, TB, 0:128], 1.0 / ROW, SHIFT,
                                            ALU.mult, ALU.add).then_inc(s_tbfree, 1)
                    if not first:
                        dve.wait_ge(s_cdma, 32 * J)
                    dve.wait_ge(s_tbfree, tb[0] + 1)
                    tb[0] = tb[0] + 1
                    nc.vector.tensor_copy(chi[:, :], crow[:, :]).then_inc(s_chi, 1)
                    dve.wait_ge(s_chi, J + 1)
                    nc.vector.tensor_tensor(clo[:, :], crow[:, :], chi[:, :], ALU.subtract).then_inc(s_clo, 1)

                def parts(j, u):
                    n = (b * NJ + j) * UNITS + u
                    table = SUB_LAST if isinstance(j, int) and j >= NJ - 2 else SUB
                    if table[u] == "D":
                        dve.wait_ge(s_p32, n + 1)
                        nc.vector.tensor_tensor(p2[:, u % NB, :], p32[:, u % NB, :], p1[:, u % NB, :],
                                                ALU.subtract).then_inc(s_subd, 1)

                def scale_sums(J):
                    dve.wait_ge(s_bc, J + 1)
                    nc.vector.tensor_tensor(onrm[:, :], osb[0:96, :], ps[0:96, TB, :],
                                            ALU.mult).then_inc(s_on, 1)
                    dve.wait_ge(s_on, START + J + 1)
                    dve.sem_inc(s_tbfree, 1)

                def add_heads(j, J):
                    dve.wait_ge(s_proj, START + J + 1)
                    xs = x[:, ds((j & (NCH - 1)) * TC, TC)]
                    nc.vector.scalar_tensor_tensor(out=xs, in0=ps[:, TB, :], scalar=w("head_bias")[:, ds(j // NCH, 1)], in1=xs,
                                                   op0=ALU.add, op1=ALU.add).then_inc(s_tbfree, 1)

                tb = [None]
                dve.wait_ge(s_out, START + b * 64)
                for m in range(TILES):
                    reduce_tile(0, m)
                chunk_max(b * NJ)
                tb[0] = 1 + b * 3 * NJ
                max_rows(b * NJ, True)
                dve.wait_ge(s_cneg, b * NJ + 1)
                for m in range(TILES):
                    reduce_tile(1, m)
                parts(0, 0)

                def attend(j, first, has_next, has_max):
                    J = b * NJ + j
                    tb[0] = 1 + b * 3 * NJ + (1 if first else 2 + 3 * (j - 1))
                    if has_next:
                        chunk_max(J + 1)
                        dve.wait_ge(s_cneg, J + 2)
                    for u in range(UNITS):
                        if u + 1 < UNITS:
                            parts(j, u + 1)
                        elif has_next:
                            parts(j + 1, 0)
                        if has_max:
                            reduce_tile(j + 2, 2 * u)
                            reduce_tile(j + 2, 2 * u + 1)
                        if u == 2 and has_next:
                            max_rows(J + 1)
                        if u == 5 and not first:
                            scale_sums(J - 1)
                        if u == 9 and not first:
                            add_heads(j - 1, J - 1)
                qchunks(dve, attend)
                scale_sums(b * NJ + NJ - 1)
                add_heads(NJ - 1, b * NJ + NJ - 1)

                L2 = L0 + NCH
                centre(0, 0, L2)

                def norm2(i, par, more):
                    if more:
                        centre(i + 1, 1 - par, L2 + i + 1)
                    dve.wait_ge(s_xln, L2 + i - 1)
                    normalise(par, L2 + i)
                    dve.wait_ge(s_z, L2 + i + 1)
                    nc.vector.tensor_scalar(xln2[:, ds(i * TC, TC)], z[:, par, :], vec("ln2_w"), vec("ln2_b"),
                                            ALU.mult, ALU.add).then_inc(s_xln, 1)
                chunks(dve, norm2)

                def mlp(i, par, more):
                    G = b * NCH + i
                    dve.wait_ge(s_fc2, TWO + G + 1)
                    nc.vector.scalar_tensor_tensor(
                        out=x2[:, ds(i * ROWS + 1, ROWS), 1:SIDE + 1],
                        in0=ps[:, FC2, :].rearrange("p (r w) -> p r w", r=ROWS), scalar=vec("fc2_b"),
                        in1=x[:, ds(i * TC, TC)].rearrange("p (r w) -> p r w", r=ROWS),
                        op0=ALU.add, op1=ALU.add).then_inc(s_x2, 1)
                chunks(dve, mlp)

                Q0 = b * NQ

                def front_d(f):
                    FQ = Q0 + f
                    dve.wait_ge(s_dtp, FQ + 1)
                    nc.vector.tensor_scalar(mdt[:, :], ps[:, SA, :], vec("dt_b"), 30.0, ALU.add,
                                            ALU.min).then_inc(s_m, 1)

                def front_r(f):
                    FQ = Q0 + f
                    dve.wait_ge(s_bc1, FQ + 1)
                    nc.vector.tensor_tensor(rbc[:, :], ps[:, SB, :], bc1[:, :],
                                            ALU.subtract).then_inc(s_rbc, 1)

                def front_e(f):
                    dve.wait_ge(s_l, Q0 + f + 1)
                    nc.vector.scalar_tensor_tensor(out=dts[:, :], in0=ps[:, SA, :], scalar=vec("dt_b"), in1=ldt[:, :],
                                                   op0=ALU.add, op1=ALU.max).then_inc(s_dt, 1)

                def first_parts(f):
                    FQ = Q0 + f
                    dve.wait_ge(s_dt, FQ + 1)
                    dve.wait_ge(s_rbc, FQ + 1)
                    dve.wait_ge(s_xcs, FQ + 1)
                    nc.vector.tensor_tensor(us[:, :], dts[:, :], slot(xcs, f), ALU.mult).then_inc(s_parts, 1)
                    if not (isinstance(f, int) and f == 0):
                        dve.wait_ge(s_stk, 16 * 12 * FQ)
                    nc.vector.tensor_copy(part_of("bc", 0), bc1[:, :])
                    nc.vector.tensor_copy(part_of("bc", 1), rbc[:, :])
                    nc.vector.tensor_copy(part_of("dt", 0), dts[:, :])
                    dve.wait_ge(s_parts, FQ * 4 + 1)
                    nc.vector.tensor_copy(part_of("u", 0), us[:, :]).then_inc(s_parts, 1)

                def remainders(f):
                    dve.wait_ge(s_parts, (Q0 + f) * 4 + 2)
                    nc.vector.tensor_tensor(rdt[:, :], dts[:, :], part_of("dt", 0), ALU.subtract)
                    nc.vector.tensor_tensor(ru[:, :], us[:, :], part_of("u", 0), ALU.subtract)
                    nc.vector.tensor_tensor(part_of("bc", 2), rbc[:, :], part_of("bc", 1),
                                            ALU.subtract).then_inc(s_parts, 1)

                def last_parts(f):
                    dve.wait_ge(s_parts, (Q0 + f) * 4 + 3)
                    nc.vector.tensor_copy(part_of("dt", 1), rdt[:, :])
                    nc.vector.tensor_copy(part_of("u", 1), ru[:, :]).then_inc(s_parts, 1)
                    dve.wait_ge(s_parts, (Q0 + f) * 4 + 4)
                    nc.vector.tensor_tensor(part_of("dt", 2), rdt[:, :], part_of("dt", 1), ALU.subtract)
                    nc.vector.tensor_tensor(part_of("u", 2), ru[:, :], part_of("u", 1),
                                            ALU.subtract).then_inc(s_pcs, 1)

                def scan_group(q, g, first, between=None):
                    Q = Q0 + q
                    for k in range(4):
                        dve.wait_ge(s_uu, Q * 16 + g * 4 + k + 1)
                        if g == 0:
                            dve.wait_ge(s_bcev, Q * 8 + 1 + k)
                        b2 = bsb[:, TC * k:TC * k + TC].rearrange("p (t n) -> p t n", t=2)
                        nc.vector.tensor_tensor(tn(dbx[:, g % 2, :], k),
                                                ps[:, UU + k % 2, :].rearrange("p (t n) -> p t n", t=2),
                                                b2, ALU.mult).then_inc(s_dbx, 1)
                    if between is not None:
                        front_d(between)
                    dve.wait_ge(s_dbx, Q * 16 + g * 4 + 4)
                    dve.wait_ge(s_da, Q * 16 + g * 4 + 4)
                    if g == 0 and first:
                        dve.wait_ge(s_dz, b + 1)
                    if g >= 2:
                        dve.wait_ge(s_hc, Q * GR + g - 1)
                    elif not first:
                        dve.wait_ge(s_hc, Q * GR + g - 1)
                    nc.vector.tensor_tensor_scan(hs[:, g % 2, :], dA[:, g % 2, :], dbx[:, g % 2, :], 0.0, ALU.mult,
                                                 ALU.add).then_inc(s_scan, 1)

                def gate(q):
                    Q = Q0 + q
                    dve.wait_ge(s_y, (Q + 1) * GR)
                    nc.vector.scalar_tensor_tensor(
                        out=ya[:, :], in0=slot(xcs, q), scalar=vec("D"), in1=ps[:, YB, :], op0=ALU.mult, op1=ALU.add).then_inc(s_ya, 1)
                    dve.wait_ge(s_ya, Q + 1)
                    dve.wait_ge(s_outp, START + Q)
                    nc.vector.tensor_tensor(ym[:, :], ya[:, :], slot(szs, q), ALU.mult).then_inc(s_ym, 1)

                for f in range(2):
                    front_d(f)
                    front_r(f)
                    front_e(f)
                    if f == 0:
                        first_parts(0)
                        remainders(0)
                        last_parts(0)

                def scan_chunk(q, first, has_front, has_next, has_out):
                    scan_group(q, 0, first)
                    if has_next:
                        first_parts(q + 1)
                        remainders(q + 1)
                        last_parts(q + 1)
                    scan_group(q, 1, first)
                    if not first:
                        gate(q - 1)
                    scan_group(q, 2, first)
                    scan_group(q, 3, first, q + 2 if has_front else None)
                    if has_front:
                        front_r(q + 2)
                        front_e(q + 2)
                mchunks(dve, scan_chunk)
                Q = Q0 + NQ - 1
                dve.wait_ge(s_scan, (Q + 1) * GR)
                dve.wait_ge(s_bcev, Q * 8 + 8)
                dve.wait_ge(s_y, Q * GR + GR - 2)
                states_times_c(nc.vector, GR - 1).then_inc(s_hcd, 1)
                gate(NQ - 1)

                dve.wait_ge(s_gmm, b + 1)
                nc.vector.tensor_reduce(gs[:, 1:2], ps[:, SB, 0:NQ], AX.X, ALU.add, negate=True).then_inc(s_gmu, 1)
                dve.wait_ge(s_grs, b + 1)
                nc.vector.tensor_scalar(gs[:, 5:6], gs[:, 4:5], vec("gn_w"), None, ALU.mult).then_inc(s_gsc2, 1)
                dve.wait_ge(s_gsc2, b + 1)
                nc.vector.scalar_tensor_tensor(out=gs[:, 6:7], in0=gs[:, 1:2], scalar=gs[:, 5:6], in1=vec("gn_b"),
                                               op0=ALU.mult, op1=ALU.add).then_inc(s_gsc, 1)
                for n in range(4):
                    dve.wait_ge(s_gxp, b * 4 + n + 1)
                    rows = fin[:, 1024 * n:1024 * n + 1024].rearrange("p (r w) -> p r w", r=16)
                    nc.vector.tensor_tensor(rows, rows,
                                            x2[:, 16 * n + 1:16 * n + 17, 1:SIDE + 1], ALU.add).then_inc(s_fin, 1)

        @block.gpsimd
        def _(pool):
            def affine(par, L, norm):
                pool.wait_ge(s_z, L + 1)
                pool.sem_inc(s_seen, 1)
                nc.gpsimd.tensor_scalar(xln[:, par, :], z[:, par, :], vec(f"ln{norm}_w"), vec(f"ln{norm}_b"),
                                        ALU.mult, ALU.add).then_inc(s_xln, 1)
            pool.sem_inc(s_v3, START)
            pool.wait_ge(s_cst, 16)
            def ones_of_k():
                nc.gpsimd.memset(kst[96:128, :], ROW).then_inc(s_fill, 1)

            def ones_of_v():
                nc.gpsimd.memset(vst[:, :].rearrange("p (n m) -> p n m", m=128)[:, :, 96:128],
                                 1.0).then_inc(s_fill, 1)
            ones_of_k()
            with pool.Fori(0, B) as b:
                L0 = b * 2 * NCH
                pool.wait_ge(s_fill, 2 * b + 1)
                affine(0, L0, 1)
                pool.wait_ge(s_xln, L0 + 1)
                pool.sem_inc(s_seen, 1)
                ones_of_v()
                pool.wait_ge(s_fill, 2 * b + 2)
                pool.sem_inc(s_seen, 1)

                def qkv(i, par, more):
                    G = b * NCH + i
                    if more:
                        affine(1 - par, L0 + i + 1, 1)
                    pool.wait_ge(s_vr, START + G + 1)
                    pool.sem_inc(s_seen, 1)
                    nc.gpsimd.tensor_copy(v_part(1, i), vres4()).then_inc(s_v2, 1)
                    pool.wait_ge(s_v2, G + 1)
                    nc.gpsimd.tensor_tensor(v_part(2, i), vres4(), v_part(1, i), ALU.subtract).then_inc(s_v3, 1)
                chunks(pool, qkv)

                def weights(j, J):
                    pool.wait_ge(s_proj, START + J)
                    pool.sem_inc(s_seen, 1)
                    nc.gpsimd.tensor_copy(pcur[:, :], w("proj")[0:96, ds((j & (NJ - NCH)) * (128 // NCH), 128)]).then_inc(s_pcur, 1)

                def attend(j, first, has_next, has_max):
                    J = b * NJ + j
                    for u in range(UNITS):
                        if u == 1 and not first:
                            weights(j - 1, J - 1)
                        if (SUB if has_max else SUB_LAST)[u] == "P":
                            pool.wait_ge(s_p32, J * UNITS + u + 1)
                            nc.gpsimd.tensor_tensor(p2[:, u % NB, :], p32[:, u % NB, :], p1[:, u % NB, :],
                                                    ALU.subtract).then_inc(s_subp, 1)
                qchunks(pool, attend)
                weights(NJ - 1, b * NJ + NJ - 1)
                pool.wait_ge(s_x2, START + (b + 1) * NCH)
                pool.sem_inc(s_seen, 1)
                nc.gpsimd.memset(dA[:, :, :].rearrange("p a (n t) -> p (a n) t", t=L)[:, :, 0:1], 0.0).then_inc(s_dz, 1)

                def scan_chunk(q, first, has_front, has_next, has_out):
                    Q = b * NQ + q
                    last = isinstance(q, int) and q == NQ - 1
                    pool.wait_ge(s_bcev, Q * 8 + 8)
                    for g in range(GR - 1 if last else GR):
                        pool.wait_ge(s_scan, Q * GR + g + 1)
                        if not (first and g < 2):
                            pool.wait_ge(s_y, Q * GR + g - 1)
                        states_times_c(nc.gpsimd, g).then_inc(s_hc, 1)
                    if last:
                        pool.wait_ge(s_hc, (Q + 1) * GR - 1)
                        pool.sem_inc(s_hc, 1)
                mchunks(pool, scan_chunk)

                pool.wait_ge(s_y, (b + 1) * (NQ * GR))
                pool.sem_inc(s_seen, 1)
                ones_of_k()

        @block.sync
        def _(sp):
            sp.dma_start(cst[:, :], consts_in).then_inc(s_cst, 16)
            sp.dma_start(raw[:, :], raw_in).then_inc(s_raw, 16)
            sp.sem_inc(s_out, START)

            def load(b, n):
                rows = x_in[ds(b, 1), :, 16 * n:16 * n + 16, :] if not isinstance(b, int) else \
                    x_in[b:b + 1, :, 16 * n:16 * n + 16, :]
                sp.dma_start(x[:, 1024 * n:1024 * n + 1024],
                             rows.rearrange("a c h w -> c (a h w)")).then_inc(s_x if n else s_x0, 16)
            for n in range(4):
                load(0, n)

            def send_rows(j, J):
                sp.wait_ge(s_clo, J + 1)
                sp.sem_inc(s_step, 1)
                for n, part in enumerate((chi, clo)):
                    dst = qst[96 + n:97 + n, ds(j * TC, TC)]
                    sp.dma_start(dst, part[:, :]).then_inc(s_cdma, 16)

            def send_parts(f, Q0):
                FQ = Q0 + f
                sp.wait_ge(s_pcs, FQ + 1)
                if not (isinstance(f, int) and f < 2):
                    sp.wait_ge(s_uu, (FQ - 1) * 16)
                sp.sem_inc(s_step, 1)
                to = stk.rearrange("p a n -> p (a n)")
                width = len(KINDS) * COLS
                for part in range(PARTS):
                    for t in range(4):
                        dst = to[32 * part:32 * part + 32, ds((f & 1) * width, width)]
                        dst = dst.rearrange("p (h t n) -> p h t n", h=2 * len(KINDS), t=4)[:, :, t, :]
                        src = pcs[32 * t:32 * t + 32, part, :].rearrange("p (h n) -> p h n", h=2 * len(KINDS))
                        sp.dma_start(dst, src).then_inc(s_stk, 16)

            def image(b, last):
                send_rows(0, b * NJ)
                with sp.Fori(1, NJ) as j:
                    send_rows(j, b * NJ + j)
                send_parts(0, b * NQ)
                send_parts(1, b * NQ)
                with sp.Fori(2, NQ) as f:
                    send_parts(f, b * NQ)
                for n in range(4):
                    if not last:
                        sp.wait_ge(s_gxp, 4 * b + n + 1)
                        sp.sem_inc(s_step, 1)
                        load(b + 1, n)
                    sp.wait_ge(s_fin, 4 * b + n + 1)
                    sp.sem_inc(s_step, 1)
                    sp.dma_start(out[ds(b, 1), :, 16 * n:16 * n + 16, :].rearrange("a c h w -> c (a h w)"),
                                 fin[:, 1024 * n:1024 * n + 1024]).then_inc(s_out, 16)
            if B > 1:
                with sp.Fori(0, B - 1) as b:
                    image(b, False)
            image(B - 1, True)
            sp.wait_ge(s_out, START + B * 64)


def layout(inp):
    g = {k: np.asarray(v) for k, v in inp.items()}
    L0 = lambda k: g["L0_conv_" + k]
    parts = {}
    parts["mean"] = np.full((128, 128), 1.0 / C, np.float32)
    parts["ident"] = np.eye(128, dtype=np.float32)
    qkv = L0("qkv_w")
    for n, k in enumerate(("wq", "wk")):
        t = qkv[128 * n:128 * n + 128].T.reshape(C, HEADS, 1, HD)
        parts[k] = np.broadcast_to(t, (C, HEADS, 3, HD)).reshape(C, 384)
    parts["wv"] = qkv[256:384].T
    pw = L0("proj_w").T.reshape(HEADS, HD, C).transpose(1, 0, 2).reshape(1, HD, 512)
    parts["proj"] = np.concatenate([np.broadcast_to(pw, (3, HD, 512)).reshape(96, 512), np.zeros((32, 512), np.float32)])
    parts["spread"] = np.full((128, 128), 1.0 / 32, np.float32)
    parts["head_bias"] = np.stack([L0("proj_b")] + [np.zeros(C, np.float32)] * (HEADS - 1), 1)
    parts["w1"] = L0("fc1_w").T
    parts["w2"] = L0("fc2_w").T.reshape(2, 128, C).transpose(1, 0, 2).reshape(128, 256)
    vec = {k: L0(k) for k in ("ln1_w", "ln1_b", "ln2_w", "ln2_b", "fc2_b")}
    vec["fc1_b0"], vec["fc1_b1"] = L0("fc1_b")[:128], L0("fc1_b")[128:]
    vec["eps"] = np.full(128, EPS, np.float32)
    M = lambda k: g["L1_conv_" + k]
    parts["conv"] = M("conv_w").transpose(1, 2, 3, 0).reshape(C, 9 * C)
    in_w = M("in_proj_w")
    xi, taps, gate = (np.zeros((L, F, L, E), np.float32) for _ in range(3))
    for t in range(L):
        gate[t, :, t, :] = in_w[E:].T
        for k in range(DCONV):
            if t - (DCONV - 1) + k >= 0:
                xi[t - (DCONV - 1) + k, :, t, :] = in_w[:E].T
                taps[t - (DCONV - 1) + k, :, t, :] = M("conv1d_w")[:, 0, k]
    parts["xi"], parts["z"] = xi.reshape(128, 256), gate.reshape(128, 256)
    x_w = M("x_proj_w")
    dt_col, dt_row, bc, o_w = (np.zeros((4, E, 4, n), np.float32) for n in (E, E, 2 * ST_N, F))
    for t in range(4):
        dt_col[t, :, t, :] = x_w[0][:, None]
        dt_row[t, :, t, :] = M("dt_proj_w")[:, 0]
        bc[t, :, t, :] = x_w[1:].T
        o_w[t, :, t, :] = M("out_proj_w").T
    parts["dt"], parts["bc"], parts["out"] = dt_col.reshape(128, 128), bc.reshape(128, 128), o_w.reshape(128, 64)
    row = np.arange(128)
    parts["sum"] = (row % 32 == 8 * (row // 32) + row[:, None] // 16).astype(np.float32)
    n_group = C // GROUPS * N
    parts["group"] = np.where(row[:, None] // 32 == row // 32, np.float32(1.0 / n_group), np.float32(0))
    parts["A"] = M("A_log").reshape(GR, 128).T
    vec.update(conv_b=M("conv_b"), gn_w=M("gn_w"), gn_b=M("gn_b"), conv1d_b=np.tile(M("conv1d_b"), 4),
               dt_b=np.tile(M("dt_proj_b"), 4), D=np.tile(M("D"), 4))
    parts["vecs"] = np.stack([vec[k] for k in VECS], 1)
    wide = np.arange(512)
    of = row[:, None] % 32
    raws = {"conv1d": taps.reshape(128, 256), "dt_row": dt_row.reshape(128, 128),
            "spread_e": of == wide // 16, "spread_b": of == row % 16, "spread_c": of == 16 + row % 16}
    join = lambda d, keys: np.ascontiguousarray(np.concatenate([np.asarray(d[k], np.float32) for k in keys], 1))
    return join(parts, WIDTHS), join(raws, RAW)


def kernel(**inputs):
    import concourse.bacc as bacc
    from concourse.bass_utils import run_bass_kernel_spmd

    nc = bacc.Bacc("TRN2", target_bir_lowering=False, num_devices=1)
    x = np.ascontiguousarray(inputs["x"])
    consts, raws = layout(inputs)
    x_in = nc.dram_tensor("x_in", x.shape, F32, kind="ExternalInput").ap()
    c_in = nc.dram_tensor("consts_in", consts.shape, F32, kind="ExternalInput").ap()
    r_in = nc.dram_tensor("raw_in", raws.shape, F32, kind="ExternalInput").ap()
    out = nc.dram_tensor("out", x.shape, F32, kind="ExternalOutput").ap()
    build(nc, x_in, c_in, r_in, out, x.shape[0])
    r = run_bass_kernel_spmd(nc, [{"x_in": x, "consts_in": consts, "raw_in": raws}], core_ids=[0])
    return r.results[0]["out"]
```
